# Optimizing a Trainium2 kernel written in Bass

```python
import numpy as np
import jax
import jax.numpy as jnp

def _softmax(x, axis=-1):
    return jax.nn.softmax(x, axis=axis)

def _gelu(x):
    return jax.nn.gelu(x, approximate=True)

def _silu(x):
    return jax.nn.silu(x)

def _sigmoid(x):
    return jax.nn.sigmoid(x)

def _layernorm(x, axis=-1, eps=1e-05):
    m = jnp.mean(x, axis=axis, keepdims=True)
    v = jnp.var(x, axis=axis, keepdims=True)
    return (x - m) / jnp.sqrt(v + eps)

def _scatter_add(tgt, idx, src, axis=0):
    return tgt.at[idx].add(src)

def _segment_sum(src, seg, n):
    return jax.ops.segment_sum(src, seg, n)
kernel_name = 'mk_gnn_resnorm_d4_gnn_r8_0006fc'

def setup_inputs(seed: int=0):
    np.random.seed(seed)
    _w = jnp.asarray

    def _rec_inputs():
        import jax
        import jax.numpy as jnp
        _gk = jax.random.key(seed)
        x = -0.0003713 + 1 * jax.random.normal(jax.random.fold_in(_gk, 1), (6250, 128), jnp.float32)
        _s = jax.random.randint(jax.random.fold_in(_gk, 2), (50000,), 0, 6250, jnp.int32)
        _d = jax.random.randint(jax.random.fold_in(_gk, 3), (50000,), 0, 6250, jnp.int32)
        _loop = jnp.arange(6250, dtype=jnp.int32)
        src = jnp.concatenate([_s, _d, _loop])
        dst = jnp.concatenate([_d, _s, _loop])
        _o = jnp.argsort(dst, stable=True)
        src = src[_o]
        dst = dst[_o]
        edge_weight = jax.random.uniform(jax.random.fold_in(_gk, 13), (106250,), jnp.float32, 0.0, 1)
        return (x, src, dst, edge_weight)
    x, src, dst, edge_weight = _rec_inputs()

    def _L0_gnn_setup():
        import jax, jax.numpy as jnp
        import numpy as np
        N = 12500
        E = 100000
        D = 128
        key = jax.random.key(seed)
        ks = jax.random.split(key, 12)
        s = lambda fan_in: 1.0 / np.sqrt(fan_in)
        return {'h': jax.random.normal(ks[0], (N, D), dtype=jnp.float32), 'w': jax.random.uniform(ks[1], (E,), dtype=jnp.float32), 'src': jax.random.randint(ks[2], (E,), 0, N, dtype=jnp.int32), 'dst': jax.random.randint(ks[3], (E,), 0, N, dtype=jnp.int32), 'W1': jax.random.uniform(ks[4], (2 * D + 1, D), jnp.float32, -s(2 * D + 1), s(2 * D + 1)), 'b1': jnp.zeros((D,), jnp.float32), 'W2': jax.random.uniform(ks[5], (D, D), jnp.float32, -s(D), s(D)), 'b2': jnp.zeros((D,), jnp.float32), 'U1': jax.random.uniform(ks[6], (2 * D, D), jnp.float32, -s(2 * D), s(2 * D)), 'c1': jnp.zeros((D,), jnp.float32), 'U2': jax.random.uniform(ks[7], (D, D), jnp.float32, -s(D), s(D)), 'c2': jnp.zeros((D,), jnp.float32)}
    _L0_gnn_all = _L0_gnn_setup()
    _L0_gnn_in = {k: v for k, v in _L0_gnn_all.items() if k in ('W1', 'b1', 'W2', 'b2', 'U1', 'c1', 'U2', 'c2')}
    del _L0_gnn_all

    def _L1_gnn_setup():
        import jax, jax.numpy as jnp
        import numpy as np
        N_VAR, N_FAC, N_EDGE, D = (12500, 6250, 125000, 128)
        key = jax.random.key(seed)
        ks = jax.random.split(key, 8)
        return {'variables': jax.random.normal(ks[0], (N_VAR, D), dtype=jnp.float32), 'factors': jax.random.normal(ks[1], (N_FAC, D), dtype=jnp.float32), 'senders': jax.random.randint(ks[2], (N_EDGE,), 0, N_VAR), 'receivers': jax.random.randint(ks[3], (N_EDGE,), 0, N_FAC), 'Wm': jax.random.normal(ks[4], (2 * D, D), dtype=jnp.float32) * (1.0 / np.sqrt(2 * D)), 'bm': jnp.zeros((D,), dtype=jnp.float32), 'Wc': jax.random.normal(ks[5], (2 * D, D), dtype=jnp.float32) * (1.0 / np.sqrt(2 * D)), 'bc': jnp.zeros((D,), dtype=jnp.float32)}
    _L1_gnn_all = _L1_gnn_setup()
    _L1_gnn_in = {k: v for k, v in _L1_gnn_all.items() if k in ('factors', 'Wm', 'bm', 'Wc', 'bc')}
    del _L1_gnn_all

    def _L2_gnn_setup():
        import jax, jax.numpy as jnp
        import numpy as np
        N = 6250
        E = 100000
        F_IN = 128
        HEADS = 4
        OUT_PER_HEAD = 32
        NEG_SLOPE = 0.2

        def _leaky_relu(v, slope):
            return jnp.where(v >= 0, v, slope * v)
        key = jax.random.key(seed)
        k1, k2, k3, k4, k5 = jax.random.split(key, 5)
        x = jax.random.normal(k1, (N, F_IN), dtype=jnp.float32)
        edge_index = jax.random.randint(k2, (2, E), 0, N, dtype=jnp.int64)
        limW = float(np.sqrt(6.0 / (F_IN + OUT_PER_HEAD)))
        W = jax.random.uniform(k3, (HEADS, F_IN, OUT_PER_HEAD), jnp.float32, -limW, limW)
        lima = float(np.sqrt(6.0 / (OUT_PER_HEAD + 1)))
        a_l = jax.random.uniform(k4, (HEADS, OUT_PER_HEAD), jnp.float32, -lima, lima)
        a_r = jax.random.uniform(k5, (HEADS, OUT_PER_HEAD), jnp.float32, -lima, lima)
        return {'x': x, 'edge_index': edge_index, 'W': W, 'a_l': a_l, 'a_r': a_r}
    _L2_gnn_all = _L2_gnn_setup()
    _L2_gnn_in = {k: v for k, v in _L2_gnn_all.items() if k in ('W', 'a_l', 'a_r')}
    del _L2_gnn_all

    def _L3_gnn_setup():
        import jax, jax.numpy as jnp
        import numpy as np
        N_NODES = 12500
        N_EDGES = 200000
        IN_FEAT = 128
        HID_FEAT = 128
        OUT_FEAT = 128

        def _mean_aggregate(h, src, dst, num_nodes):
            msgs = h[src]
            summed = jax.ops.segment_sum(msgs, dst, num_segments=num_nodes)
            deg = jax.ops.segment_sum(jnp.ones((src.shape[0],), h.dtype), dst, num_segments=num_nodes)
            deg = jnp.maximum(deg, 1.0)
            return summed / deg[:, None]
        key = jax.random.key(seed)
        k1, k2, k3, k4, k5 = jax.random.split(key, 5)
        x = jax.random.normal(k1, (N_NODES, IN_FEAT), dtype=jnp.float32)
        W_in = jax.random.normal(k2, (2, IN_FEAT, HID_FEAT), dtype=jnp.float32) * (1.0 / np.sqrt(IN_FEAT))
        W_out = jax.random.normal(k3, (2, HID_FEAT, OUT_FEAT), dtype=jnp.float32) * (1.0 / np.sqrt(HID_FEAT))
        src = jax.random.randint(k4, (N_EDGES,), 0, N_NODES, dtype=jnp.int32)
        dst = jax.random.randint(k5, (N_EDGES,), 0, N_NODES, dtype=jnp.int32)
        return {'x': x, 'W_in': W_in, 'W_out': W_out, 'src': src, 'dst': dst}
    _L3_gnn_all = _L3_gnn_setup()
    _L3_gnn_in = {k: v for k, v in _L3_gnn_all.items() if k in ('W_in', 'W_out')}
    del _L3_gnn_all
    return {'x': x, 'src': src, 'dst': dst, 'edge_weight': edge_weight, 'L0_gnn_W1': _L0_gnn_in['W1'], 'L0_gnn_b1': _L0_gnn_in['b1'], 'L0_gnn_W2': _L0_gnn_in['W2'], 'L0_gnn_b2': _L0_gnn_in['b2'], 'L0_gnn_U1': _L0_gnn_in['U1'], 'L0_gnn_c1': _L0_gnn_in['c1'], 'L0_gnn_U2': _L0_gnn_in['U2'], 'L0_gnn_c2': _L0_gnn_in['c2'], 'L1_gnn_factors': _L1_gnn_in['factors'], 'L1_gnn_Wm': _L1_gnn_in['Wm'], 'L1_gnn_bm': _L1_gnn_in['bm'], 'L1_gnn_Wc': _L1_gnn_in['Wc'], 'L1_gnn_bc': _L1_gnn_in['bc'], 'L2_gnn_W': _L2_gnn_in['W'], 'L2_gnn_a_l': _L2_gnn_in['a_l'], 'L2_gnn_a_r': _L2_gnn_in['a_r'], 'L3_gnn_W_in': _L3_gnn_in['W_in'], 'L3_gnn_W_out': _L3_gnn_in['W_out']}

def reference(x, src, dst, edge_weight, L0_gnn_W1, L0_gnn_b1, L0_gnn_W2, L0_gnn_b2, L0_gnn_U1, L0_gnn_c1, L0_gnn_U2, L0_gnn_c2, L1_gnn_factors, L1_gnn_Wm, L1_gnn_bm, L1_gnn_Wc, L1_gnn_bc, L2_gnn_W, L2_gnn_a_l, L2_gnn_a_r, L3_gnn_W_in, L3_gnn_W_out):
    import jax
    import jax.numpy as jnp

    def _L0_gnn_ref(h, w, src, dst, W1, b1, W2, b2, U1, c1, U2, c2):
        import jax, jax.numpy as jnp
        import numpy as np
        N = 12500
        E = 100000
        D = 128
        n = h.shape[0]
        msg_in = jnp.concatenate([h[src], h[dst], w[:, None]], axis=1)
        msg = jax.nn.relu(msg_in @ W1 + b1) @ W2 + b2
        agg = jax.ops.segment_max(msg, dst, num_segments=n)
        deg = jax.ops.segment_sum(jnp.ones((dst.shape[0],), jnp.int32), dst, num_segments=n)
        agg = jnp.where((deg > 0)[:, None], agg, jnp.zeros((), h.dtype))
        upd_in = jnp.concatenate([h, agg], axis=1)
        return jax.nn.relu(upd_in @ U1 + c1) @ U2 + c2

    def _L1_gnn_ref(variables, factors, senders, receivers, Wm, bm, Wc, bc):
        import jax, jax.numpy as jnp
        import numpy as np
        N_VAR, N_FAC, N_EDGE, D = (12500, 6250, 125000, 128)
        x_i = variables[senders]
        x_j = factors[receivers]
        x = jnp.concatenate([x_i, x_j], axis=-1)
        msg = jax.nn.relu(x @ Wm + bm)
        agg = jax.ops.segment_sum(msg, senders, num_segments=variables.shape[0])
        h = jnp.concatenate([variables, agg], axis=-1)
        h = jax.nn.relu(h @ Wc + bc)
        return variables + h

    def _L2_gnn_ref(x, edge_index, W, a_l, a_r):
        import jax, jax.numpy as jnp
        import numpy as np
        N = 6250
        E = 100000
        F_IN = 128
        HEADS = 4
        OUT_PER_HEAD = 32
        NEG_SLOPE = 0.2

        def _leaky_relu(v, slope):
            return jnp.where(v >= 0, v, slope * v)
        src, dst = (edge_index[0], edge_index[1])
        n = x.shape[0]
        Wh = jnp.einsum('nf,kfh->knh', x, W)
        e_l = jnp.einsum('knh,kh->kn', Wh, a_l)
        e_r = jnp.einsum('knh,kh->kn', Wh, a_r)
        e = _leaky_relu(e_l[:, src] + e_r[:, dst], NEG_SLOPE)
        seg_max = jax.vmap(lambda ee: jax.ops.segment_max(ee, dst, num_segments=n))(e)
        seg_max = jnp.maximum(seg_max, -1000000000.0)
        exp_e = jnp.exp(e - seg_max[:, dst])
        denom = jax.vmap(lambda ee: jax.ops.segment_sum(ee, dst, num_segments=n))(exp_e)
        alpha = exp_e / (denom[:, dst] + 1e-16)
        weighted = alpha[..., None] * Wh[:, src, :]
        out = jax.vmap(lambda w: jax.ops.segment_sum(w, dst, num_segments=n))(weighted)
        return out.transpose(1, 0, 2).reshape(n, -1)

    def _L3_gnn_ref(x, W_in, W_out, src, dst):
        import jax, jax.numpy as jnp
        import numpy as np
        N_NODES = 12500
        N_EDGES = 200000
        IN_FEAT = 128
        HID_FEAT = 128
        OUT_FEAT = 128

        def _mean_aggregate(h, src, dst, num_nodes):
            msgs = h[src]
            summed = jax.ops.segment_sum(msgs, dst, num_segments=num_nodes)
            deg = jax.ops.segment_sum(jnp.ones((src.shape[0],), h.dtype), dst, num_segments=num_nodes)
            deg = jnp.maximum(deg, 1.0)
            return summed / deg[:, None]
        n = x.shape[0]
        neigh = _mean_aggregate(x, src, dst, n)
        h = x @ W_in[0] + neigh @ W_in[1]
        h = jax.nn.relu(h)
        neigh = _mean_aggregate(h, src, dst, n)
        h = h @ W_out[0] + neigh @ W_out[1]
        return h
    edge_index = jnp.stack([src, dst])
    x = _layernorm(x + _L0_gnn_ref(x, edge_weight, src, dst, L0_gnn_W1, L0_gnn_b1, L0_gnn_W2, L0_gnn_b2, L0_gnn_U1, L0_gnn_c1, L0_gnn_U2, L0_gnn_c2), axis=-1)
    x = _layernorm(x + _L1_gnn_ref(x, L1_gnn_factors, src, dst, L1_gnn_Wm, L1_gnn_bm, L1_gnn_Wc, L1_gnn_bc), axis=-1)
    x = _layernorm(x + _L2_gnn_ref(x, edge_index, L2_gnn_W, L2_gnn_a_l, L2_gnn_a_r), axis=-1)
    x = _layernorm(x + _L3_gnn_ref(x, L3_gnn_W_in, L3_gnn_W_out, src, dst), axis=-1)
    return x

_drawn_inputs = setup_inputs


def setup_inputs(seed=0):
    import zlib

    import numpy as np

    out = dict(_drawn_inputs(seed))
    spreads = {'L0_gnn_b1': (0.0, 0.8),
     'L0_gnn_b2': (0.0, 0.455),
     'L0_gnn_c1': (0.0, 0.1),
     'L0_gnn_c2': (0.0, 0.1),
     'L1_gnn_bm': (0.0, 0.1),
     'L1_gnn_bc': (0.0, 0.375)}
    factors = {'edge_weight': 43.106, 'L0_gnn_W1': 2.922}
    for name, (base, spread) in spreads.items():
        noise = np.random.default_rng([zlib.crc32(name.encode()), seed]).standard_normal(out[name].shape)
        drawn = base * np.exp(spread * noise) if base else spread * noise
        out[name] = jnp.asarray(drawn.astype(out[name].dtype))
    for name, factor in factors.items():
        out[name] = (out[name] * factor).astype(out[name].dtype)
    return out
```

```python
from contextlib import ExitStack

import concourse.bass as bass
from concourse import mybir


P = 128
E = 106250
N = 6250
F = 128
HEADS = 4
HID = F // HEADS
EB = 512
CT = EB // P
NB = -(-E // EB)
NB += -NB % CT
EP = NB * EB
T = EP // P
TC = -(-T // P)
TL = T - (TC - 1) * P
NG = -(-N // EB)
NT = NG * CT
NP = NT * P
SLOTS = 4
BIG = 3.0e38
FAR = 1.0e6
LN_EPS = 1e-5

ALU = mybir.AluOpType
ACT = mybir.ActivationFunctionType
F32 = mybir.dt.float32
BF16 = mybir.dt.bfloat16
I32 = mybir.dt.int32


def steps(eng, n, unroll, *pieces):
    last = max(lag for lag, _ in pieces)
    head = -(-(last + unroll) // unroll) * unroll
    main = max(head, n - n % unroll)

    def alone(i):
        for lag, f in pieces:
            if 0 <= i - lag < n:
                f((i - lag) // unroll, (i - lag) % unroll)

    for i in range(min(head, n + last)):
        alone(i)
    if main > head:
        with eng.Fori(head // unroll, main // unroll) as r:
            for u in range(unroll):
                for lag, f in pieces:
                    d = u - lag
                    f(r + d // unroll if d // unroll else r, d % unroll)
    for i in range(main, n + last):
        alone(i)


def gnn_program(nc, a, out):
    ctx = ExitStack()

    def sb(name, shape, dt=F32):
        return ctx.enter_context(nc.sbuf_tensor(name, shape, dt))

    def ps(name):
        return ctx.enter_context(nc.psum_tensor(name, [P, EB], F32))

    def sem(name):
        return ctx.enter_context(nc.semaphore(name))

    def dram(name, shape, dt=F32):
        return nc.dram_tensor(name, shape, dt, kind="Internal").ap()

    with ctx:
        meta_d = dram("edge_meta", [3, EP], BF16)
        weight_d = dram("edge_weight_padded", [1, EP])
        dst_d = dram("dst_rows", [T, P])
        last_dst_d = dram("tile_last_dst", [1, T])
        start_d = dram("row_start", [1, NP + P])
        first_d = dram("receiver_rows", [EP, F])
        recv_d = dram("receiver_table", [NP, F])
        send_d = dram("sender_table", [NP, F])
        factor_d = dram("factor_table", [NP, F])
        att_d = dram("attention_table", [NP, F + HEADS])
        scan_d = dram("scan_rows", [EP, F])
        att_scan_d = dram("attention_scan_rows", [EP, F + HEADS])

        ident = sb("ident", [P, P])
        x_nm = sb("x_nm", [P, NT, F])
        xT = sb("xT", [P, NP])
        src_cols = sb("src_cols", [P, T], I32)
        rank_cols = sb("rank_cols", [P, T])
        first_dst = sb("first_dst", [P, TC], I32)
        start_i = sb("start_i", [P, NT], I32)
        end_i = sb("end_i", [P, NT], I32)
        mask = sb("mask", [P, NT])
        inv_deg = sb("inv_deg", [P, NT])
        eps = sb("eps", [P, 1])
        sel = sb("sel", [P, HEADS])

        w1 = sb("w1", [P, 2, F]); w1w = sb("w1w", [1, F]); b1 = sb("b1", [P, 1])
        w2 = sb("w2", [P, F]); b2 = sb("b2", [P, F])
        u1 = sb("u1", [P, 2, F]); c1 = sb("c1", [P, 1]); u2 = sb("u2", [P, F]); c2 = sb("c2", [P, F])
        wm = sb("wm", [P, 2, F]); bm = sb("bm", [P, 1]); wc = sb("wc", [P, 2, F]); bc = sb("bc", [P, 1])
        wh = sb("wh", [P, HEADS, HID]); al = sb("al", [P, F]); ar = sb("ar", [P, F])
        w_in = sb("w_in", [P, 2, F]); w_out = sb("w_out", [P, 2, F])

        idx = [sb(f"idx{s}", [P, CT], I32) for s in range(SLOTS)]
        gath = [sb(f"gath{s}", [P, CT, F + HEADS]) for s in range(SLOTS)]
        recv = [sb(f"recv{s}", [P, CT, F]) for s in range(SLOTS)]
        meta = [sb(f"meta{s}", [P, 3, EB], BF16) for s in range(SLOTS)]
        wrow = [sb(f"wrow{s}", [1, EB]) for s in range(SLOTS)]
        rows = [sb(f"rows{s}", [P, CT, F + HEADS]) for s in range(SLOTS)]
        same = [sb(f"same{s}", [P, CT, P]) for s in range(2)]
        hid = [sb(f"hid{s}", [P, EB]) for s in range(2)]
        scan = [sb(f"scan{s}", [P, EB]) for s in range(2)]
        den = [sb(f"den{s}", [P, EB]) for s in range(2)]
        run_max = [sb(f"run_max{s}", [P, EB + 1]) for s in range(2)]
        score = [sb(f"score{s}", [P, EB]) for s in range(2)]
        below = [sb(f"below{s}", [P, EB]) for s in range(2)]
        drop = [sb(f"drop{s}", [P, EB]) for s in range(2)]
        x_new = [sb(f"x_new{s}", [P, CT, F]) for s in range(2)]
        stats = sb("stats", [P, CT, 6]); mv = sb("mv", [P, CT, 2]); std = sb("std", [P, CT]); rstd = sb("rstd", [P, CT])
        head_sum = sb("head_sum", [P, CT * HEADS])
        bank = [ps(f"bank{k}") for k in range(8)]
        agg, aggT, y_nm, prod = recv[0:2], scan, recv[2:4], score
        xT_new, recv_o, firsts = den, same, gath

        v_done = sem("v_done")
        a_done = sem("a_done")
        node_got = [sem(f"node_got{s}") for s in range(2)]
        scattered = [sem(f"scattered{s}") for s in range(2)]
        firsts_got = sem("firsts_got")
        n_idx = sem("n_idx")
        n_gath_free = sem("n_gath_free")
        n_agg = sem("n_agg")
        n_agg_free = sem("n_agg_free")
        n_agg_turned = sem("n_agg_turned")
        n_aggT = sem("n_aggT")
        n_hid_ps = sem("n_hid_ps")
        n_hid = sem("n_hid")
        n_rows_ps = sem("n_rows_ps")
        n_rows_free = sem("n_rows_free")
        n_var = sem("n_var")
        n_std = sem("n_std")
        n_x = sem("n_x")
        n_x_turned_a = sem("n_x_turned_a")
        n_x_turned_v = sem("n_x_turned_v")
        n_x_bank_free = sem("n_x_bank_free")
        n_xT_new = sem("n_xT_new")
        n_tab_ps = sem("n_tab_ps")
        n_recv_ps = sem("n_recv_ps")
        n_bank_free = {7: sem("n_bank7_free"), 5: sem("n_bank5_free")}
        n_heads = sem("n_heads")
        n_tab = sem("n_tab")
        n_recv = sem("n_recv")
        n_recv_sc = sem("n_recv_sc")
        n_stored = [sem(f"n_stored{s}") for s in range(2)]
        n_recv_stored = [sem(f"n_recv_stored{s}") for s in range(2)]
        n_recv_all = sem("n_recv_all")
        n_scat_all = sem("n_scat_all")
        n_first_out = sem("n_first_out")
        n_load = sem("n_load"); n_load_ready = sem("n_load_ready")
        out_done = sem("out_done")

        gathered = [sem(f"gathered{s}") for s in range(SLOTS)]
        e_idx = sem("e_idx")
        e_gath_free = sem("e_gath_free")
        recv_in = [sem(f"recv_in{s}") for s in range(SLOTS)]
        meta_in = [sem(f"meta_in{s}") for s in range(SLOTS)]
        e_recv_free = sem("e_recv_free")
        e_meta_free = sem("e_meta_free")
        e_same = sem("e_same"); e_same_free = sem("e_same_free")
        e_pre = sem("e_pre"); e_pre_free = sem("e_pre_free")
        e_hid = sem("e_hid"); e_hid_free = sem("e_hid_free")
        e_msg = sem("e_msg"); e_msg_free = sem("e_msg_free")
        e_scan = sem("e_scan"); e_scan_free = sem("e_scan_free")
        e_back = sem("e_back"); e_back_free = sem("e_back_free")
        e_rows = sem("e_rows")
        stored = [sem(f"stored{s}") for s in range(SLOTS)]
        e_den_free = sem("e_den_free")
        e_er = sem("e_er"); e_er_free = sem("e_er_free")
        e_rep = sem("e_rep"); e_rep_free = sem("e_rep_free")
        e_idx_free = sem("e_idx_free")
        e_below = sem("e_below"); e_exp = sem("e_exp")

        with ExitStack() as pctx:
            def psb(name, shape, dt=F32):
                return pctx.enter_context(nc.sbuf_tensor(name, shape, dt))

            dst_r = psb("dst_r", [P, TC, P], I32)
            src_r = psb("src_r", [P, TC, P], I32)
            prev_r = psb("prev_r", [P, TC], I32)
            dst_f = psb("dst_f", [P, TC, P])
            src_f = psb("src_f", [P, TC, P])
            prev_f = psb("prev_f", [P, TC])
            goes = psb("goes", [P, TC, P], BF16)
            bar = psb("bar", [P, TC, P], BF16)
            begins = psb("begins", [P, TC, P])
            rank_f = psb("rank_f", [P, TC, P])
            rank_b = psb("rank_b", [P, TC, P], BF16)
            zeros = psb("zeros", [P, EP * F // P // 32])
            node_i = psb("node_i", [P, NT], I32)
            node_f = psb("node_f", [P, NT])
            tail = psb("tail", [1, P])
            lasts = psb("lasts", [P, T])
            junk = psb("junk", [P, T])
            tiles = psb("tiles", [P, NT])
            tiles_i = psb("tiles_i", [P, NT], I32)
            inside = psb("inside", [P, NT])
            start_f = psb("start_f", [P, NT])
            end_f = psb("end_f", [P, NT])
            lone = psb("lone", [P, NT])
            start_t = psb("start_t", [NT, P])
            end_t = psb("end_t", [NT, P])
            found = xT[:, :].rearrange("p (t k) -> p t k", k=P)

            filled = sem("prep_filled"); zeroed = sem("prep_zeroed"); zero_ready = sem("prep_zero_ready")
            loaded = sem("prep_loaded"); ident_done = sem("ident_done")
            marked = sem("prep_marked"); written = sem("prep_written"); turned = sem("prep_turned")
            rows_f_ready = sem("prep_rows_f_ready"); p_done = sem("p_done"); turn_free = sem("prep_turn_free")
            dst_written = sem("prep_dst_written"); lasts_in = sem("prep_lasts_in"); tiles_ready = sem("prep_tiles_ready")
            found_in = sem("prep_found_in"); start_ready = sem("prep_start_ready"); start_out = sem("prep_start_out")
            start_written = sem("prep_start_written"); end_in = sem("prep_end_in"); back_ready = sem("prep_back_ready")
            weights_in = sem("weights_in")

            full = (TC - 1) * P
            rest = E // P - full
            left = E % P
            with nc.Block() as block:
                @block.sync
                def _(sp):
                    sp.wait_ge(filled, 3)
                    sp.sem_inc(filled, -3)
                    for r, t in ((dst_r, a["dst"]), (src_r, a["src"])):
                        sp.dma_start(r[:, 0:TC - 1, :], t[0:full * P].rearrange("(c p k) -> p c k", p=P, k=P)).then_inc(loaded, 16)
                        sp.dma_start(r[0:rest, TC - 1, :], t[full * P:(full + rest) * P].rearrange("(p k) -> p k", k=P)).then_inc(loaded, 16)
                        sp.dma_start(r[rest:rest + 1, TC - 1, 0:left], t[E - left:E].rearrange("(p k) -> p k", p=1)).then_inc(loaded, 16)
                    with nc.allow_non_contiguous_dma("one word of each tile"):
                        for c in range(TC):
                            lo, n = (1, P - 1) if c == 0 else (0, P if c < TC - 1 else rest + 1)
                            first = (c * P + lo - 1) * P
                            sp.dma_start(prev_r[lo:lo + n, c:c + 1],
                                         a["dst"][first:first + n * P].rearrange("(p k) -> p k", k=P)[:, P - 1:P]).then_inc(loaded, 16)
                    for t, src in ((w1[:, 0, :], a["L0_gnn_W1"][0:F, :]), (w1[:, 1, :], a["L0_gnn_W1"][F:2 * F, :]),
                                   (w1w[:, :], a["L0_gnn_W1"][2 * F:2 * F + 1, :]),
                                   (b1[:, :], a["L0_gnn_b1"].rearrange("(p o) -> p o", o=1)),
                                   (w2[:, :], a["L0_gnn_W2"]), (b2[:, :], a["L0_gnn_b2"].partition_broadcast(P)),
                                   (u1[:, :, :], a["L0_gnn_U1"].rearrange("(t p) n -> p t n", p=P)),
                                   (c1[:, :], a["L0_gnn_c1"].rearrange("(p o) -> p o", o=1)),
                                   (u2[:, :], a["L0_gnn_U2"]), (c2[:, :], a["L0_gnn_c2"].partition_broadcast(P)),
                                   (wm[:, :, :], a["L1_gnn_Wm"].rearrange("(t p) n -> p t n", p=P)),
                                   (bm[:, :], a["L1_gnn_bm"].rearrange("(p o) -> p o", o=1)),
                                   (wc[:, :, :], a["L1_gnn_Wc"].rearrange("(t p) n -> p t n", p=P)),
                                   (bc[:, :], a["L1_gnn_bc"].rearrange("(p o) -> p o", o=1)),
                                   (wh[:, :, :], a["L2_gnn_W"].rearrange("k f h -> f k h")),
                                   (al[:, :], a["L2_gnn_a_l"].rearrange("k h -> (k h)").partition_broadcast(P)),
                                   (ar[:, :], a["L2_gnn_a_r"].rearrange("k h -> (k h)").partition_broadcast(P)),
                                   (w_in[:, :, :], a["L3_gnn_W_in"].rearrange("t p n -> p t n")),
                                   (w_out[:, :, :], a["L3_gnn_W_out"].rearrange("t p n -> p t n"))):
                        sp.dma_start(t, src).then_inc(weights_in, 16)
                    sp.wait_ge(marked, 1)
                    sp.sem_inc(marked, -1)
                    for c in range(TC):
                        n = P if c < TC - 1 else TL
                        at = slice(c * P * P, (c * P + n) * P)
                        sp.dma_start(dst_d[c * P:c * P + n, :], dst_f[0:n, c, :]).then_inc(dst_written, 16)
                        with nc.allow_non_contiguous_dma("one word of each tile"):
                            sp.dma_start(last_dst_d[0, c * P:c * P + n].rearrange("(p o) -> p o", o=1),
                                         dst_f[0:n, c, P - 1:P]).then_inc(dst_written, 16)
                        for m, r in enumerate((goes, rank_b, bar)):
                            sp.dma_start(meta_d[m, at].rearrange("(p k) -> p k", k=P), r[0:n, c, :]).then_inc(written, 16)
                    sp.dma_start(weight_d[0:1, E:EP], zeros[0:1, 0:EP - E]).then_inc(written, 16)
                    sp.dma_start(weight_d[0, 0:E].rearrange("(p k) -> p k", k=1250), a["edge_weight"].rearrange("(p k) -> p k", k=1250)).then_inc(written, 16)
                    sp.wait_ge(dst_written, 32 * TC)
                    sp.sem_inc(dst_written, -32 * TC)
                    sp.dma_start(lasts[:, :], last_dst_d[0, :].partition_broadcast(P)).then_inc(lasts_in, 16)
                    sp.wait_ge(start_out, 1)
                    sp.sem_inc(start_out, -1)
                    sp.dma_start(start_d[0, 0:NP].rearrange("(t p) -> t p", p=P), start_t[:, :]).then_inc(start_written, 16)
                    sp.dma_start(start_d[0:1, NP:NP + P], tail[:, :]).then_inc(start_written, 16)
                    sp.wait_ge(start_written, 32)
                    sp.sem_inc(start_written, -32)
                    sp.dma_start(end_t[:, :], start_d[0, 1:NP + 1].rearrange("(t p) -> t p", p=P)).then_inc(end_in, 16)
                    sp.wait_ge(written, 16 * (3 * TC + 2))
                    sp.sem_inc(written, -(16 * (3 * TC + 2)))
                    sp.wait_ge(weights_in, 16 * 19)
                    sp.sem_inc(weights_in, -16 * 19)
                    for free, n in ((n_gath_free, 2), (n_agg_free, 2), (n_rows_free, 2), (n_x_bank_free, 1), (n_bank_free[7], 1), (n_bank_free[5], 1),
                                    (e_gath_free, SLOTS), (e_recv_free, SLOTS), (e_meta_free, SLOTS), (e_same_free, 2),
                                    (e_pre_free, 2), (e_hid_free, 2), (e_msg_free, 2), (e_scan_free, 2), (e_back_free, 2),
                                    (e_er_free, 1), (e_den_free, 1), (e_rep_free, 2)):
                        sp.sem_inc(free, n)

                @block.scalar
                def _(act):
                    act.wait_ge(zero_ready, 1)
                    act.sem_inc(zero_ready, -1)
                    z = first_d.rearrange("(p k r) f -> k p (r f)", p=P, k=32)
                    for k in range(32):
                        act.dma_start(z[k], zeros[:, :]).then_inc(zeroed, 16)
                    act.wait_ge(zeroed, 16 * 32)
                    act.sem_inc(zeroed, -16 * 32)

                @block.gpsimd
                def _(pool):
                    pool.memset(dst_r[:, TC - 1, :], N).then_inc(filled, 1)
                    pool.memset(src_r[:, TC - 1, :], 0).then_inc(filled, 1)
                    pool.memset(prev_r[:, 1:TC], N).then_inc(p_done, 1)
                    pool.memset(prev_r[:, 0:1], -1).then_inc(p_done, 1)
                    pool.memset(ident[:, :], 0.0).then_inc(p_done, 1)
                    pool.memset(eps[:, :], LN_EPS).then_inc(p_done, 1)
                    pool.memset(sel[:, :], 0.0).then_inc(p_done, 1)
                    pool.memset(tail[:, :], float(EP)).then_inc(p_done, 1)
                    pool.iota(node_i[:, :], pattern=[[P, NT]], base=0, channel_multiplier=1).then_inc(p_done, 1)
                    pool.wait_ge(p_done, 7)
                    pool.sem_inc(p_done, -7)
                    pool.sem_inc(filled, 1)
                    pool.affine_select(out=ident[:, :], in_=ident[:, :], compare_op=ALU.not_equal, fill=1.0, base=0,
                                       pattern=[[-1, P]], channel_multiplier=1).then_inc(ident_done, 1)
                    pool.affine_select(out=sel[:, :], in_=sel[:, :], compare_op=ALU.not_equal, fill=1.0, base=0,
                                       pattern=[[-HID, HEADS]], channel_multiplier=1).then_inc(ident_done, 1)
                    pool.wait_ge(tiles_ready, 1)
                    pool.sem_inc(tiles_ready, -1)
                    for t in range(NT):
                        pool.indirect_dma_start(out=found[:, t, :], out_offset=None, in_=dst_d[:, :],
                                                in_offset=bass.IndirectOffsetOnAxis(ap=tiles_i[:, t:t + 1], axis=0),
                                                bounds_check=T - 1, oob_is_err=False).then_inc(found_in, 16)

                @block.vector
                def _(v):
                    def chain(ins):
                        ins.then_inc(v_done, 1)
                        v.wait_ge(v_done, 1)
                        v.sem_inc(v_done, -1)

                    for s in range(2):
                        chain(v.memset(run_max[s][:, :], 0.0))
                        chain(v.memset(scan[s][:, :], 0.0))
                        chain(v.memset(den[s][:, :], 0.0))
                    chain(v.memset(zeros[:, :], 0.0))
                    v.sem_inc(zero_ready, 1)
                    v.wait_ge(loaded, 16 * (6 + TC))
                    v.tensor_copy(dst_f[:, :, :], dst_r[:, :, :]).then_inc(v_done, 1)
                    v.tensor_copy(prev_f[:, :], prev_r[:, :]).then_inc(v_done, 1)
                    v.tensor_copy(first_dst[:, :], dst_r[:, :, 0]).then_inc(v_done, 1)
                    v.tensor_copy(node_f[:, :], node_i[:, :]).then_inc(v_done, 1)
                    v.wait_ge(v_done, 4)
                    v.sem_inc(v_done, -4)
                    v.tensor_tensor(goes[:, :, 1:P], dst_f[:, :, 1:P], dst_f[:, :, 0:P - 1], ALU.is_equal).then_inc(v_done, 1)
                    v.tensor_tensor(goes[:, :, 0], dst_f[:, :, 0], prev_f[:, :], ALU.is_equal).then_inc(v_done, 1)
                    v.wait_ge(v_done, 2)
                    v.sem_inc(v_done, -2)
                    chain(v.tensor_scalar(bar[:, :, :], goes[:, :, :], -1.0, BIG, ALU.add, ALU.mult))
                    chain(v.tensor_scalar(begins[:, :, :], goes[:, :, :], -1.0, 1.0, ALU.mult, ALU.add))
                    chain(v.memset(begins[:, :, 0:1], 0.0))
                    for c in range(TC):
                        v.tensor_tensor_scan(rank_f[:, c, :], begins[:, c, :], begins[:, c, :], 0.0, ALU.add, ALU.max).then_inc(v_done, 1)
                    v.wait_ge(v_done, TC)
                    v.sem_inc(v_done, -TC)
                    chain(v.tensor_copy(rank_b[:, :, :], rank_f[:, :, :]))
                    v.sem_inc(marked, 1)
                    chain(v.tensor_copy(src_f[:, :, :], src_r[:, :, :]))
                    v.sem_inc(rows_f_ready, 1)
                    for c in range(TC):
                        n = P if c < TC - 1 else TL
                        v.wait_ge(turned, 1)
                        v.sem_inc(turned, -1)
                        v.tensor_copy(src_cols[:, c * P:c * P + n], bank[c % 2][:, 0:n])
                        v.tensor_copy(rank_cols[:, c * P:c * P + n], bank[c % 2][:, P:P + n]).then_inc(turn_free, 1)
                    v.wait_ge(lasts_in, 16)
                    with v.Fori(0, NT) as t:
                        v.tensor_scalar(junk[:, :], lasts[:, :], node_f[:, bass.ds(t, 1)], None, ALU.is_lt, ALU.add,
                                        accum_out=tiles[:, bass.ds(t, 1)]).then_inc(v_done, 1)
                        v.wait_ge(v_done, 1)
                        v.sem_inc(v_done, -1)
                    chain(v.tensor_scalar(tiles[:, :], tiles[:, :], float(T - 1), None, ALU.min))
                    chain(v.tensor_copy(tiles_i[:, :], tiles[:, :]))
                    v.sem_inc(tiles_ready, 1)
                    v.wait_ge(found_in, 16 * NT)
                    with v.Fori(0, NT) as t:
                        v.tensor_scalar(junk[:, 0:P], found[:, bass.ds(t, 1), :], node_f[:, bass.ds(t, 1)], None, ALU.is_lt, ALU.add,
                                        accum_out=inside[:, bass.ds(t, 1)]).then_inc(v_done, 1)
                        v.wait_ge(v_done, 1)
                        v.sem_inc(v_done, -1)
                    chain(v.scalar_tensor_tensor(start_f[:, :], tiles[:, :], float(P), inside[:, :], ALU.mult, ALU.add))
                    v.sem_inc(start_ready, 1)
                    v.wait_ge(turned, 1)
                    v.sem_inc(turned, -1)
                    chain(v.tensor_copy(start_t[:, :], bank[2][0:NT, 0:P]))
                    v.sem_inc(start_out, 1)
                    v.wait_ge(turned, 1)
                    v.sem_inc(turned, -1)
                    chain(v.tensor_copy(end_f[:, :], bank[3][:, 0:NT]))
                    chain(v.tensor_tensor(lone[:, :], end_f[:, :], start_f[:, :], ALU.subtract))
                    chain(v.tensor_scalar(mask[:, :], lone[:, :], 1.0, None, ALU.min))
                    chain(v.tensor_scalar(inv_deg[:, :], lone[:, :], 1.0, None, ALU.max))
                    chain(v.reciprocal(inv_deg[:, :], inv_deg[:, :]))
                    chain(v.tensor_tensor(inv_deg[:, :], inv_deg[:, :], mask[:, :], ALU.mult))
                    chain(v.tensor_scalar(end_f[:, :], end_f[:, :], -1.0, 0.0, ALU.add, ALU.max))
                    chain(v.tensor_copy(end_i[:, :], end_f[:, :]))
                    chain(v.tensor_scalar(lone[:, :], mask[:, :], -FAR, FAR, ALU.mult, ALU.add))
                    chain(v.tensor_tensor(lone[:, :], lone[:, :], start_f[:, :], ALU.add))
                    chain(v.tensor_copy(start_i[:, :], lone[:, :]))

                @block.tensor
                def _(pe):
                    pe.wait_ge(ident_done, 2)
                    pe.wait_ge(rows_f_ready, 1)
                    pe.sem_inc(rows_f_ready, -1)
                    for c in range(TC):
                        if c >= 2:
                            pe.wait_ge(turn_free, 1)
                            pe.sem_inc(turn_free, -1)
                        pe.transpose(bank[c % 2][:, 0:P], src_f[:, c, :], ident[:, :])
                        pe.transpose(bank[c % 2][:, P:2 * P], rank_f[:, c, :], ident[:, :]).then_inc(turned, 1)
                    pe.wait_ge(start_ready, 1)
                    pe.sem_inc(start_ready, -1)
                    pe.transpose(bank[2][0:NT, 0:P], start_f[:, :], ident[:, :]).then_inc(turned, 1)
                    pe.wait_ge(end_in, 16)
                    pe.sem_inc(end_in, -16)
                    pe.transpose(bank[3][:, 0:NT], end_t[:, :], ident[0:NT, 0:NT]).then_inc(turned, 1)
                    pe.wait_ge(turn_free, 2)
                    pe.sem_inc(turn_free, -2)

        started = {"node": 0, "scatter": 0, "firsts": 0, "edge": 0}

        def part(q, s, unroll, n):
            lo = q * (unroll * n) + s * n
            return slice(lo, lo + n) if isinstance(q, int) else bass.ds(lo, n)

        def node_phase(k):
            gathers = 1 <= k <= 5
            dense = k in (1, 2, 4, 5)
            norm = k in (1, 2, 3, 5)
            turn = k in (0, 1, 2, 3, 6)
            makes_recv = k in (0, 1, 2)
            by_matmul = k in (0, 1, 2, 6)
            wx, wa = {1: (u1[:, 0, :], u1[:, 1, :]), 2: (wc[:, 0, :], wc[:, 1, :]), 4: (w_in[:, 0, :], w_in[:, 1, :]),
                      5: (w_out[:, 0, :], w_out[:, 1, :])}.get(k, (None, None))
            back = u2 if k == 1 else ident
            w_tab = {0: w1[:, 0, :], 2: wh[:, :, :].rearrange("p k h -> p (k h)"), 6: wm[:, 1, :]}.get(k)
            w_recv = {0: w1[:, 1, :], 1: wm[:, 0, :]}.get(k)
            width = F + HEADS if k == 3 else F
            from_d = att_scan_d if k == 3 else scan_d
            to_d = {0: send_d, 2: att_d, 3: send_d, 4: send_d, 6: factor_d}.get(k)
            to_w = F + HEADS if k == 2 else F
            agg_ps, hid_ps, rows_ps, x_ps, tab_ps = bank[0:2], bank[2:4], bank[4:6], bank[6], bank[7]
            recv_bank = 5 if k == 0 else 7
            late = 3 if dense else 1
            got_before, scattered_before, firsts_before = started["node"], started["scatter"], started["firsts"]
            groups = [(NG + 1 - s) // 2 for s in range(2)]

            with nc.Block() as block:
                @block.gpsimd
                def _(pool):
                    def gather(q, s):
                        pool.wait_ge(n_gath_free, 1)
                        pool.sem_inc(n_gath_free, -1)
                        pool.tensor_copy(idx[s][:, :], end_i[:, part(q, s, 2, CT)]).then_inc(n_idx, 1)
                        pool.wait_ge(n_idx, 1)
                        pool.sem_inc(n_idx, -1)
                        for c in range(CT):
                            pool.indirect_dma_start(out=gath[s][:, c, 0:width], out_offset=None, in_=from_d[:, :],
                                                    in_offset=bass.IndirectOffsetOnAxis(ap=idx[s][:, c:c + 1], axis=0),
                                                    bounds_check=EP - 1, oob_is_err=False).then_inc(node_got[s], 16)

                    def scatter(q, s):
                        pool.wait_ge(n_recv_sc, 1)
                        pool.sem_inc(n_recv_sc, -1)
                        pool.tensor_copy(idx[2 + s][:, :], start_i[:, part(q, s, 2, CT)]).then_inc(n_idx, 1)
                        pool.wait_ge(n_idx, 1)
                        pool.sem_inc(n_idx, -1)
                        for c in range(CT):
                            pool.indirect_dma_start(out=first_d[:, :],
                                                    out_offset=bass.IndirectOffsetOnAxis(ap=idx[2 + s][:, c:c + 1], axis=0),
                                                    in_=recv_o[s][:, c, :], in_offset=None,
                                                    bounds_check=EP - 1, oob_is_err=False).then_inc(scattered[s], 16)

                    work = [(0, gather)] * gathers + [(7 if gathers else 0, scatter)] * makes_recv
                    if work:
                        steps(pool, NG, 2, *work)
                    if makes_recv:
                        pool.wait_ge(n_recv_all, 1)
                        pool.sem_inc(n_recv_all, -1)
                        for c in range(TC):
                            pool.indirect_dma_start(out=firsts[c % SLOTS][:, c // SLOTS, 0:F], out_offset=None, in_=recv_d[:, :],
                                                    in_offset=bass.IndirectOffsetOnAxis(ap=first_dst[:, c:c + 1], axis=0),
                                                    bounds_check=NP - 1, oob_is_err=False).then_inc(firsts_got, 16)

                @block.sync
                def _(sp):
                    if k in (0, 6):
                        sp.wait_ge(n_load_ready, 1)
                        sp.sem_inc(n_load_ready, -1)
                        x_in, whole = (a["x"] if k == 0 else a["L1_gnn_factors"]), N // P
                        sp.dma_start(x_nm[:, 0:whole, :], x_in[0:whole * P, :].rearrange("(t p) f -> p t f", p=P)).then_inc(n_load, 16)
                        sp.dma_start(x_nm[0:N - whole * P, whole, :], x_in[whole * P:N, :]).then_inc(n_load, 16)

                    def store_table(q, s):
                        sp.wait_ge(n_tab, 1)
                        sp.sem_inc(n_tab, -1)
                        rows_d = to_d[part(q, s, 2, EB), :].rearrange("(t p) f -> p t f", p=P)
                        rows_s = {3: x_new, 4: y_nm}.get(k, rows)[s][:, :, 0:to_w]
                        sp.dma_start(rows_d, rows_s).then_inc(n_stored[s], 16)

                    def store_receivers(q, s):
                        sp.wait_ge(n_recv, 1)
                        sp.sem_inc(n_recv, -1)
                        sp.dma_start(recv_d[part(q, s, 2, EB), :].rearrange("(t p) f -> p t f", p=P), recv_o[s][:, :, :]).then_inc(n_recv_stored[s], 16)

                    work = [(0, store_table)] * (to_d is not None) + [(0, store_receivers)] * makes_recv
                    if work:
                        steps(sp, NG, 2, *work)
                    if makes_recv:
                        sp.wait_ge(n_scat_all, 1)
                        sp.sem_inc(n_scat_all, -1)
                        sp.wait_ge(firsts_got, 16 * (firsts_before + TC))
                        by_tile = first_d.rearrange("(t e) f -> t e f", e=P)
                        for c in range(TC):
                            n = P if c < TC - 1 else TL
                            sp.dma_start(by_tile[c * P:c * P + n, 0, :], firsts[c % SLOTS][0:n, c // SLOTS, 0:F]).then_inc(n_first_out, 16)
                        sp.wait_ge(n_first_out, 16 * TC)
                        sp.sem_inc(n_first_out, -16 * TC)
                    if k == 5:
                        sp.wait_ge(n_tab, NG)
                        sp.sem_inc(n_tab, -NG)
                        whole = N // P
                        sp.dma_start(out[0:whole * P, :].rearrange("(t p) f -> p t f", p=P), x_nm[:, 0:whole, :]).then_inc(out_done, 16)
                        sp.dma_start(out[whole * P:N, :], x_nm[0:N - whole * P, whole, :]).then_inc(out_done, 16)
                        sp.wait_ge(out_done, 32)

                @block.vector
                def _(v):
                    def chain(ins, n=1):
                        ins.then_inc(v_done, 1)
                        v.wait_ge(v_done, n)
                        v.sem_inc(v_done, -n)

                    def tiled(t):
                        return t[:, :].rearrange("p (t f) -> p t f", f=F)

                    if k in (0, 6):
                        chain(v.memset(x_nm[:, N // P:NT, :], 0.0))
                        v.sem_inc(n_load_ready, 1)
                        v.wait_ge(n_load, 32)
                        v.sem_inc(n_load, -32)

                    def aggregate(q, s):
                        if dense:
                            v.wait_ge(n_agg_free, 1)
                            v.sem_inc(n_agg_free, -1)
                        v.wait_ge(node_got[s], (q + 1) * (16 * CT) + 16 * CT * got_before * groups[s])
                        tile_mask = mask[:, part(q, s, 2, CT)].unsqueeze(2)
                        g, o = gath[s][:, :, 0:F], agg[s][:, :, :]
                        if k == 1:
                            chain(v.tensor_tensor(o, g, b2[:, :].unsqueeze(1).to_broadcast([P, CT, F]), ALU.add))
                            chain(v.tensor_tensor(o, o, tile_mask.to_broadcast([P, CT, F]), ALU.mult))
                        elif k == 3:
                            h = head_sum[:, :].rearrange("p (t h) -> p t h", h=HEADS)
                            chain(v.tensor_scalar(h, gath[s][:, :, F:F + HEADS], 1e-16, None, ALU.add))
                            chain(v.reciprocal(h, h))
                            chain(v.tensor_tensor(h, h, tile_mask.to_broadcast([P, CT, HEADS]), ALU.mult))
                            for c in range(CT):
                                ins = v.tensor_tensor(o[:, c, :].rearrange("p (h d) -> p h d", h=HEADS), g[:, c, :].rearrange("p (h d) -> p h d", h=HEADS),
                                                      h[:, c, :].unsqueeze(2).to_broadcast([P, HEADS, HID]), ALU.mult)
                                ins.then_inc(v_done, 1)
                            v.wait_ge(v_done, CT)
                            v.sem_inc(v_done, -CT)
                        else:
                            if k in (4, 5):
                                tile_mask = inv_deg[:, part(q, s, 2, CT)].unsqueeze(2)
                            chain(v.tensor_tensor(o, g, tile_mask.to_broadcast([P, CT, F]), ALU.mult))
                        v.sem_inc(n_gath_free, 1)
                        if dense:
                            v.sem_inc(n_agg, 1)

                    def update(q, s):
                        x, y, new = x_nm[:, part(q, s, 2, CT), :], y_nm[s][:, :, :], x_new[s][:, :, :]
                        if not gathers:
                            chain(v.tensor_copy(new, x))
                            v.sem_inc(n_x, 1)
                            return
                        if k == 4 and not (isinstance(q, int) and q == 0):
                            v.wait_ge(n_stored[s], 16)
                            v.sem_inc(n_stored[s], -16)
                        if dense:
                            v.wait_ge(n_rows_ps, 1)
                            v.sem_inc(n_rows_ps, -1)
                        r = tiled(rows_ps[s])
                        if k == 1:
                            chain(v.tensor_tensor(y, r, c2[:, :].unsqueeze(1).to_broadcast([P, CT, F]), ALU.add))
                            chain(v.tensor_tensor(y, x, y, ALU.add))
                        elif k == 2:
                            chain(v.tensor_tensor(y, x, r, ALU.add))
                            chain(v.tensor_tensor(y, x, y, ALU.add))
                        elif k == 3:
                            chain(v.tensor_tensor(y, x, agg[s][:, :, :], ALU.add))
                        elif k == 4:
                            chain(v.tensor_copy(y, r))
                            v.sem_inc(n_tab, 1)
                        else:
                            chain(v.tensor_tensor(y, x, r, ALU.add))
                        if dense:
                            v.sem_inc(n_rows_free, 1)
                        if not norm:
                            return
                        for c in range(CT):
                            v.bn_stats(stats[:, c, :], y[:, c, :]).then_inc(v_done, 1)
                        v.wait_ge(v_done, CT)
                        v.sem_inc(v_done, -CT)
                        for c in range(CT):
                            v.bn_aggr(mv[:, c, :], stats[:, c, :]).then_inc(n_var, 1)
                        v.wait_ge(n_std, 1)
                        v.sem_inc(n_std, -1)
                        chain(v.reciprocal(rstd[:, :], std[:, :]))
                        if k == 3 and not (isinstance(q, int) and q == 0):
                            v.wait_ge(n_stored[s], 16)
                            v.sem_inc(n_stored[s], -16)
                        for c in range(CT):
                            v.tensor_scalar(new[:, c, :], y[:, c, :], mv[:, c, 0:1], rstd[:, c:c + 1], ALU.subtract, ALU.mult).then_inc(v_done, 1)
                        v.wait_ge(v_done, CT)
                        v.sem_inc(v_done, -CT)
                        if turn:
                            v.sem_inc(n_x, 1)
                        chain(v.tensor_copy(x, new))
                        if k in (3, 5):
                            v.sem_inc(n_tab, 1)

                    def keep_xT(q, s):
                        v.wait_ge(n_x_turned_v, 1)
                        v.sem_inc(n_x_turned_v, -1)
                        chain(v.tensor_copy(xT[:, part(q, s, 2, EB)], xT_new[s][:, :]))

                    def receivers(q, s):
                        if not (isinstance(q, int) and q == 0):
                            v.wait_ge(n_recv_stored[s], 16)
                            v.sem_inc(n_recv_stored[s], -16)
                            v.wait_ge(scattered[s], q * (16 * CT) + 16 * CT * scattered_before * groups[s])
                        if k != 2:
                            v.wait_ge(n_recv_ps, 1)
                            v.sem_inc(n_recv_ps, -1)
                            chain(v.tensor_copy(recv_o[s][:, :, :], tiled(bank[recv_bank])))
                            v.sem_inc(n_bank_free[recv_bank], 1)
                        else:
                            v.wait_ge(n_heads, 1)
                            v.sem_inc(n_heads, -1)
                            p3 = prod[s][:, :].rearrange("p (t f) -> p t f", f=F)
                            for w in (al, ar):
                                chain(v.tensor_tensor(p3, rows[s][:, :, 0:F], w[:, :].unsqueeze(1).to_broadcast([P, CT, F]), ALU.mult))
                                chain(v.reduce_sum(head_sum[:, :], prod[s][:, :].rearrange("p (g d) -> p g d", d=HID), mybir.AxisListType.X))
                                if w is al:
                                    chain(v.tensor_copy(rows[s][:, :, F:F + HEADS], head_sum[:, :].rearrange("p (t h) -> p t h", h=HEADS)))
                                else:
                                    chain(v.tensor_copy(recv_o[s][:, :, :].rearrange("p t (h d) -> p (t h) d", d=HID),
                                                        head_sum[:, :].unsqueeze(2).to_broadcast([P, CT * HEADS, HID])))
                            v.sem_inc(n_tab, 1)
                        v.sem_inc(n_recv, 1)
                        v.sem_inc(n_recv_sc, 1)

                    work = [(0, aggregate)] * gathers + [(late, update)] + [(late + 1, keep_xT)] * turn + [(late + 2, receivers)] * makes_recv
                    steps(v, NG, 2, *work)
                    if k in (3, 4):
                        for s in range(2):
                            v.wait_ge(n_stored[s], 16)
                            v.sem_inc(n_stored[s], -16)
                    if makes_recv:
                        for s in range(2):
                            v.wait_ge(n_recv_stored[s], 16)
                            v.sem_inc(n_recv_stored[s], -16)
                        v.sem_inc(n_recv_all, 1)
                        for s in range(2):
                            v.wait_ge(scattered[s], 16 * CT * (scattered_before + 1) * groups[s])
                        v.sem_inc(n_scat_all, 1)

                @block.scalar
                def _(act):
                    def chain(ins):
                        ins.then_inc(a_done, 1)
                        act.wait_ge(a_done, 1)
                        act.sem_inc(a_done, -1)

                    def keep_aggT(q, s):
                        act.wait_ge(n_agg_turned, 1)
                        act.sem_inc(n_agg_turned, -1)
                        act.sem_inc(n_agg_free, 1)
                        act.activation(aggT[s][:, :], agg_ps[s][:, :], ACT.Copy).then_inc(n_aggT, 1)

                    def hidden(q, s):
                        act.wait_ge(n_hid_ps, 1)
                        act.sem_inc(n_hid_ps, -1)
                        if k == 5:
                            chain(act.activation(hid[s][:, :], hid_ps[s][:, :], ACT.Copy))
                        elif k == 4:
                            chain(act.activation(hid[s][:, :], hid_ps[s][:, :], ACT.Relu))
                            chain(act.activation(xT[:, part(q, s, 2, EB)], hid_ps[s][:, :], ACT.Relu))
                        else:
                            chain(act.activation(hid[s][:, :], hid_ps[s][:, :], ACT.Relu, bias=(c1 if k == 1 else bc)[:, 0:1]))
                        act.sem_inc(n_hid, 1)

                    def deviation(q, s):
                        act.wait_ge(n_var, CT)
                        act.sem_inc(n_var, -CT)
                        act.activation(std[:, :], mv[:, :, 1], ACT.Sqrt, bias=eps[:, 0:1]).then_inc(n_std, 1)

                    def turned_x(q, s):
                        act.wait_ge(n_x_turned_a, 1)
                        act.sem_inc(n_x_turned_a, -1)
                        chain(act.activation(xT_new[s][:, :], x_ps[:, :], ACT.Copy))
                        act.sem_inc(n_x_bank_free, 1)
                        act.sem_inc(n_x_turned_v, 1)
                        if by_matmul:
                            act.sem_inc(n_xT_new, 1)

                    def table(q, s):
                        if not (isinstance(q, int) and q == 0):
                            act.wait_ge(n_stored[s], 16)
                            act.sem_inc(n_stored[s], -16)
                        act.wait_ge(n_tab_ps, 1)
                        act.sem_inc(n_tab_ps, -1)
                        chain(act.activation(rows[s][:, :, 0:F], tab_ps[:, :].rearrange("p (t f) -> p t f", f=F), ACT.Copy))
                        act.sem_inc(n_bank_free[7], 1)
                        act.sem_inc(n_heads if k == 2 else n_tab, 1)

                    work = ([(0, keep_aggT), (1, hidden)] * dense + [(late, deviation)] * norm + [(late + 1, turned_x)] * turn
                            + [(late + 2, table)] * (w_tab is not None))
                    steps(act, NG, 2, *work)
                    if w_tab is not None:
                        for s in range(2):
                            act.wait_ge(n_stored[s], 16)
                            act.sem_inc(n_stored[s], -16)

                @block.tensor
                def _(pe):
                    def turn_agg(q, s):
                        pe.wait_ge(n_agg, 1)
                        pe.sem_inc(n_agg, -1)
                        for c in range(CT):
                            ins = pe.transpose(agg_ps[s][:, c * P:(c + 1) * P], agg[s][:, c, :], ident[:, :])
                        ins.then_inc(n_agg_turned, 1)

                    def product(q, s):
                        pe.wait_ge(n_aggT, 1)
                        pe.sem_inc(n_aggT, -1)
                        pe.matmul(hid_ps[s][:, :], wa, aggT[s][:, :], start=True, stop=False)
                        pe.matmul(hid_ps[s][:, :], wx, xT[:, part(q, s, 2, EB)], start=False, stop=True).then_inc(n_hid_ps, 1)

                    def product_rows(q, s):
                        pe.wait_ge(n_hid, 1)
                        pe.sem_inc(n_hid, -1)
                        pe.wait_ge(n_rows_free, 1)
                        pe.sem_inc(n_rows_free, -1)
                        for c in range(CT):
                            ins = pe.matmul(rows_ps[s][:, c * P:(c + 1) * P], hid[s][:, c * P:(c + 1) * P], back[:, :], start=True, stop=True)
                        ins.then_inc(n_rows_ps, 1)

                    def turn_x(q, s):
                        pe.wait_ge(n_x, 1)
                        pe.sem_inc(n_x, -1)
                        pe.wait_ge(n_x_bank_free, 1)
                        pe.sem_inc(n_x_bank_free, -1)
                        for c in range(CT):
                            ins = pe.transpose(x_ps[:, c * P:(c + 1) * P], x_new[s][:, c, :], ident[:, :])
                        ins.then_inc(n_x_turned_a, 1)

                    def tables(q, s):
                        pe.wait_ge(n_xT_new, 1)
                        pe.sem_inc(n_xT_new, -1)
                        for w, b, ready in ((w_tab, 7, n_tab_ps), (w_recv, recv_bank, n_recv_ps)):
                            if w is None:
                                continue
                            pe.wait_ge(n_bank_free[b], 1)
                            pe.sem_inc(n_bank_free[b], -1)
                            for c in range(CT):
                                ins = pe.matmul(bank[b][:, c * P:(c + 1) * P], xT_new[s][:, c * P:(c + 1) * P], w, start=True, stop=True)
                            ins.then_inc(ready, 1)

                    work = ([(0, turn_agg), (1, product), (2, product_rows)] * dense + [(late + 1, turn_x)] * turn
                            + [(late + 2, tables)] * by_matmul)
                    steps(pe, NG, 2, *work)
            if gathers:
                started["node"] += 1
            if makes_recv:
                started["scatter"] += 1
                started["firsts"] += TC

        def edge_phase(k):
            expands = k <= 3
            table = {1: send_d, 2: factor_d, 3: att_d}.get(k, send_d)
            width = F + HEADS if k == 3 else F
            to_d = att_scan_d if k == 3 else scan_d
            marks = {1: (1, 3), 2: (0, 2), 3: (1, 3)}.get(k, (0, 1))
            pre_ps, msg_ps, back_ps, er_ps, den_ps = bank[0:2], bank[2:4], bank[4:6], bank[6], bank[7]
            before = started["edge"]

            rounds = NB // SLOTS

            with nc.Block() as block:
                @block.gpsimd
                def _(pool):
                    def gather(q, s):
                        pool.wait_ge(e_idx, 1)
                        pool.sem_inc(e_idx, -1)
                        pool.wait_ge(e_gath_free, 1)
                        pool.sem_inc(e_gath_free, -1)
                        for c in range(CT):
                            pool.indirect_dma_start(out=gath[s][:, c, 0:width], out_offset=None, in_=table[:, :],
                                                    in_offset=bass.IndirectOffsetOnAxis(ap=idx[s][:, c:c + 1], axis=0),
                                                    bounds_check=NP - 1, oob_is_err=False).then_inc(gathered[s], 16)

                    steps(pool, NB, SLOTS, (0, gather))

                @block.sync
                def _(sp):
                    def load(q, s):
                        sp.wait_ge(e_meta_free, 1)
                        sp.sem_inc(e_meta_free, -1)
                        lo, hi = marks
                        sp.dma_start(meta[s][:, lo:hi, :], meta_d[lo:hi, part(q, s, SLOTS, EB)].partition_broadcast(P)).then_inc(meta_in[s], 16)
                        if expands:
                            sp.wait_ge(e_recv_free, 1)
                            sp.sem_inc(e_recv_free, -1)
                            sp.dma_start(recv[s][:, :, :], first_d[part(q, s, SLOTS, EB), :].rearrange("(c p) f -> p c f", p=P)).then_inc(recv_in[s], 16)
                            if k == 1:
                                sp.dma_start(wrow[s][:, :], weight_d[:, part(q, s, SLOTS, EB)]).then_inc(recv_in[s], 16)

                    def store(q, s):
                        sp.wait_ge(e_rows, 1)
                        sp.sem_inc(e_rows, -1)
                        sp.dma_start(to_d[part(q, s, SLOTS, EB), :].rearrange("(c p) f -> p c f", p=P), rows[s][:, :, 0:width]).then_inc(stored[s], 16)

                    steps(sp, NB, SLOTS, (0, load), (5, store))

                @block.tensor
                def _(pe):
                    def senders(q, s):
                        if expands:
                            pe.wait_ge(recv_in[s], 32 if k == 1 else 16)
                            pe.sem_inc(recv_in[s], -(32 if k == 1 else 16))
                            pe.wait_ge(e_same, 1)
                            pe.sem_inc(e_same, -1)
                        if k == 3:
                            pe.wait_ge(e_er_free, 1)
                            pe.sem_inc(e_er_free, -1)
                            pe.wait_ge(gathered[s], (q + 1) * (16 * CT) + 16 * CT * rounds * before)
                            for c in range(CT):
                                ins = pe.matmul(er_ps[:, c * HEADS:(c + 1) * HEADS], same[s % 2][:, c, :], recv[s][:, c, 0:F:HID], start=True, stop=True)
                            ins.then_inc(e_er, 1)
                            return
                        pe.wait_ge(e_pre_free, 1)
                        pe.sem_inc(e_pre_free, -1)
                        pe.wait_ge(gathered[s], (q + 1) * (16 * CT) + 16 * CT * rounds * before)
                        b, g = pre_ps[s % 2], gath[s]
                        if k >= 4:
                            for c in range(CT):
                                ins = pe.transpose(b[:, c * P:(c + 1) * P], g[:, c, 0:F], ident[:, :])
                            ins.then_inc(e_pre, 1)
                            return
                        if k == 1:
                            pe.matmul(b[:, :], w1w[:, :], wrow[s][:, :], start=True, stop=False)
                        for c in range(CT):
                            o = b[:, c * P:(c + 1) * P]
                            pe.matmul(o, g[:, c, 0:F], ident[:, :], start=k != 1, stop=False)
                            ins = pe.matmul(o, recv[s][:, c, :], same[s % 2][:, c, :], start=False, stop=k != 1 or c == CT - 1)
                        ins.then_inc(e_pre, 1)

                    def turn_scores(q, s):
                        pe.wait_ge(e_rep, 1)
                        pe.sem_inc(e_rep, -1)
                        pe.wait_ge(e_pre_free, 1)
                        pe.sem_inc(e_pre_free, -1)
                        for c in range(CT):
                            ins = pe.transpose(pre_ps[s % 2][:, c * P:(c + 1) * P], hid[s % 2][:, c * P:(c + 1) * P], ident[:, :])
                        ins.then_inc(e_pre, 1)

                    def turn_wh(q, s):
                        pe.wait_ge(e_msg_free, 1)
                        pe.sem_inc(e_msg_free, -1)
                        for c in range(CT):
                            ins = pe.transpose(msg_ps[s % 2][:, c * P:(c + 1) * P], gath[s][:, c, 0:F], ident[:, :])
                        ins.then_inc(e_msg, 1)

                    def message(q, s):
                        pe.wait_ge(e_hid, 1)
                        pe.sem_inc(e_hid, -1)
                        pe.wait_ge(e_msg_free, 1)
                        pe.sem_inc(e_msg_free, -1)
                        pe.matmul(msg_ps[s % 2][:, :], w2[:, :], hid[s % 2][:, :], start=True, stop=True).then_inc(e_msg, 1)

                    def turn_back(q, s):
                        pe.wait_ge(e_scan, 1)
                        pe.sem_inc(e_scan, -1)
                        pe.wait_ge(e_back_free, 1)
                        pe.sem_inc(e_back_free, -1)
                        for c in range(CT):
                            ins = pe.transpose(back_ps[s % 2][:, c * P:(c + 1) * P], scan[s % 2][:, c * P:(c + 1) * P], ident[:, :])
                        if k == 3:
                            pe.wait_ge(e_den_free, 1)
                            pe.sem_inc(e_den_free, -1)
                            for c in range(CT):
                                ins = pe.matmul(den_ps[:, c * HEADS:(c + 1) * HEADS], den[s % 2][:, c * P:(c + 1) * P], sel[:, :], start=True, stop=True)
                        ins.then_inc(e_back, 1)

                    if k == 3:
                        steps(pe, NB, SLOTS, (0, senders), (1, turn_scores), (2, turn_wh), (4, turn_back))
                    else:
                        steps(pe, NB, SLOTS, (0, senders), *[(1, message)] * (k == 1), (3 if expands else 2, turn_back))

                @block.scalar
                def _(act):
                    def chain(ins):
                        ins.then_inc(a_done, 1)
                        act.wait_ge(a_done, 1)
                        act.sem_inc(a_done, -1)

                    def indices(q, s):
                        act.activation(idx[s][:, :], src_cols[:, part(q, s, SLOTS, CT)], ACT.Copy).then_inc(e_idx, 1)

                    def hidden(q, s):
                        act.wait_ge(e_pre, 1)
                        act.sem_inc(e_pre, -1)
                        act.sem_inc(e_gath_free, 1)
                        act.sem_inc(e_recv_free, 1)
                        act.sem_inc(e_same_free, 1)
                        act.wait_ge(e_hid_free, 1)
                        act.sem_inc(e_hid_free, -1)
                        chain(act.activation(hid[s % 2][:, :], pre_ps[s % 2][:, :], ACT.Relu, bias=(b1 if k == 1 else bm)[:, 0:1]))
                        act.sem_inc(e_pre_free, 1)
                        act.sem_inc(e_hid, 1)

                    def exps(q, s):
                        act.wait_ge(e_below, 1)
                        act.sem_inc(e_below, -1)
                        act.activation(below[s % 2][:, :], below[s % 2][:, :], ACT.Exp, scale=-1.0).then_inc(e_exp, 1)
                        act.activation(drop[s % 2][:, :], drop[s % 2][:, :], ACT.Exp, scale=-1.0).then_inc(e_exp, 1)

                    def keep_rows(q, s):
                        act.wait_ge(e_back, 1)
                        act.sem_inc(e_back, -1)
                        act.sem_inc(e_scan_free, 1)
                        if not (isinstance(q, int) and q == 0):
                            act.wait_ge(stored[s], 16)
                            act.sem_inc(stored[s], -16)
                        ins = act.activation(rows[s][:, :, 0:F], back_ps[s % 2][:, :].rearrange("p (c f) -> p c f", f=F), ACT.Copy)
                        if k == 3:
                            ins.then_inc(a_done, 1)
                            chain(act.activation(rows[s][:, :, F:F + HEADS], den_ps[:, 0:CT * HEADS].rearrange("p (c h) -> p c h", h=HEADS), ACT.Copy))
                            act.wait_ge(a_done, 1)
                            act.sem_inc(a_done, -1)
                            act.sem_inc(e_den_free, 1)
                        else:
                            chain(ins)
                        act.sem_inc(e_back_free, 1)
                        act.sem_inc(e_rows, 1)

                    def read(q, s):
                        act.wait_ge(e_idx_free, 1)
                        act.sem_inc(e_idx_free, -1)

                    first = {1: hidden, 2: hidden, 3: exps}.get(k, read)
                    steps(act, NB, SLOTS, (4, first), (0, indices), ({1: 7, 2: 7, 3: 6}.get(k, 5), keep_rows))
                    for s in range(SLOTS):
                        act.wait_ge(stored[s], 16)
                        act.sem_inc(stored[s], -16)

                @block.vector
                def _(v):
                    def chain(ins):
                        ins.then_inc(v_done, 1)
                        v.wait_ge(v_done, 1)
                        v.sem_inc(v_done, -1)

                    def same_receiver(q, s):
                        v.wait_ge(meta_in[s], 16)
                        v.sem_inc(meta_in[s], -16)
                        v.wait_ge(e_same_free, 1)
                        v.sem_inc(e_same_free, -1)
                        v.tensor_tensor(same[s % 2][:, :, :], meta[s][:, 1, :].rearrange("p (c e) -> p c e", e=P),
                                        rank_cols[:, part(q, s, SLOTS, CT)].unsqueeze(2).to_broadcast([P, CT, P]), ALU.is_equal).then_inc(e_same, 1)

                    def reduce(q, s):
                        if k >= 4:
                            v.wait_ge(meta_in[s], 16)
                            v.sem_inc(meta_in[s], -16)
                        v.wait_ge({1: e_msg, 2: e_hid}.get(k, e_pre), 1)
                        v.sem_inc({1: e_msg, 2: e_hid}.get(k, e_pre), -1)
                        if k == 1:
                            v.sem_inc(e_hid_free, 1)
                        if k >= 4:
                            v.sem_inc(e_gath_free, 1)
                            v.sem_inc(e_idx_free, 1)
                        v.wait_ge(e_scan_free, 1)
                        v.sem_inc(e_scan_free, -1)
                        src = {1: msg_ps, 2: hid}.get(k, pre_ps)[s % 2][:, :]
                        go_on = meta[s][:, 2 if k == 1 else 0, :]
                        chain(v.tensor_tensor_scan(scan[s % 2][:, :], go_on, src, scan[1 - s % 2][:, EB - 1:EB],
                                                   ALU.add if k == 1 else ALU.mult, ALU.max if k == 1 else ALU.add))
                        v.sem_inc({1: e_msg_free, 2: e_hid_free}.get(k, e_pre_free), 1)
                        v.sem_inc(e_meta_free, 1)
                        v.sem_inc(e_scan, 1)

                    def spread_scores(q, s):
                        v.wait_ge(e_er, 1)
                        v.sem_inc(e_er, -1)
                        v.sem_inc(e_recv_free, 1)
                        v.sem_inc(e_same_free, 1)
                        v.wait_ge(e_rep_free, 1)
                        v.sem_inc(e_rep_free, -1)
                        em = head_sum[:, :].rearrange("p (c h) -> p c h", h=HEADS)
                        chain(v.tensor_tensor(em, er_ps[:, 0:CT * HEADS].rearrange("p (c h) -> p c h", h=HEADS), gath[s][:, :, F:F + HEADS], ALU.add))
                        v.sem_inc(e_er_free, 1)
                        wide = head_sum[:, :].unsqueeze(2).to_broadcast([P, CT * HEADS, HID])
                        chain(v.scalar_tensor_tensor(hid[s % 2][:, :].rearrange("p (g d) -> p g d", d=HID), wide, 0.2, wide, ALU.mult, ALU.max))
                        v.sem_inc(e_rep, 1)

                    def running_max(q, s):
                        v.wait_ge(e_pre, 1)
                        v.sem_inc(e_pre, -1)
                        v.sem_inc(e_rep_free, 1)
                        sc, rm, dr = pre_ps[s % 2], run_max[s % 2], drop[s % 2]
                        chain(v.tensor_copy(rm[:, 0:1], run_max[1 - s % 2][:, EB:EB + 1]))
                        chain(v.tensor_tensor_scan(rm[:, 1:EB + 1], meta[s][:, 2, :], sc[:, :], rm[:, 0:1], ALU.add, ALU.max))
                        v.scalar_tensor_tensor(below[s % 2][:, :], rm[:, 1:EB + 1], -1e9, sc[:, :], ALU.max, ALU.subtract).then_inc(v_done, 1)
                        v.scalar_tensor_tensor(dr[:, :], rm[:, 0:EB], -1e9, meta[s][:, 2, :], ALU.max, ALU.add).then_inc(v_done, 1)
                        v.wait_ge(v_done, 2)
                        v.sem_inc(v_done, -2)
                        chain(v.scalar_tensor_tensor(dr[:, :], rm[:, 1:EB + 1], -1e9, dr[:, :], ALU.max, ALU.subtract))
                        v.sem_inc(e_pre_free, 1)
                        v.sem_inc(e_meta_free, 1)
                        v.sem_inc(e_below, 1)

                    def weigh(q, s):
                        v.wait_ge(e_exp, 2)
                        v.sem_inc(e_exp, -2)
                        v.wait_ge(e_msg, 1)
                        v.sem_inc(e_msg, -1)
                        v.sem_inc(e_gath_free, 1)
                        v.wait_ge(e_scan_free, 1)
                        v.sem_inc(e_scan_free, -1)
                        chain(v.tensor_tensor(score[s % 2][:, :], below[s % 2][:, :], msg_ps[s % 2][:, :], ALU.mult))
                        v.sem_inc(e_msg_free, 1)
                        for t, d in ((scan, score), (den, below)):
                            v.tensor_tensor_scan(t[s % 2][:, :], drop[s % 2][:, :], d[s % 2][:, :], t[1 - s % 2][:, EB - 1:EB], ALU.mult, ALU.add).then_inc(v_done, 1)
                        v.wait_ge(v_done, 2)
                        v.sem_inc(v_done, -2)
                        v.sem_inc(e_scan, 1)

                    if k == 3:
                        steps(v, NB, SLOTS, (0, same_receiver), (1, spread_scores), (2, running_max), (3, weigh))
                    elif expands:
                        steps(v, NB, SLOTS, (0, same_receiver), (2, reduce))
                    else:
                        steps(v, NB, SLOTS, (0, reduce))
            started["edge"] += 1

        node_phase(6)
        node_phase(0)
        for k in range(1, 6):
            edge_phase(k)
            node_phase(k)


_INS = ['x', 'src', 'dst', 'edge_weight', 'L0_gnn_W1', 'L0_gnn_b1', 'L0_gnn_W2', 'L0_gnn_b2', 'L0_gnn_U1', 'L0_gnn_c1',
        'L0_gnn_U2', 'L0_gnn_c2', 'L1_gnn_factors', 'L1_gnn_Wm', 'L1_gnn_bm', 'L1_gnn_Wc', 'L1_gnn_bc', 'L2_gnn_W',
        'L2_gnn_a_l', 'L2_gnn_a_r', 'L3_gnn_W_in', 'L3_gnn_W_out']


def kernel(**inputs):
    import numpy as _np
    import concourse.bacc as _bacc
    from concourse import mybir as _mybir
    from concourse.bass_utils import run_bass_kernel_spmd as _run

    nc = _bacc.Bacc("TRN2", target_bir_lowering=False, num_devices=1)
    arrays, args = {}, {}
    for name in _INS:
        array = _np.ascontiguousarray(inputs[name])
        arrays[f"in_{name}_dram"] = array
        args[name] = nc.dram_tensor(f"in_{name}_dram", array.shape, _mybir.dt.from_np(array.dtype), kind="ExternalInput").ap()
    out = nc.dram_tensor("out_0_dram", (N, F), F32, kind="ExternalOutput").ap()
    gnn_program(nc, args, out)
    r = _run(nc, [arrays], core_ids=[0])
    return r.results[0]["out_0_dram"]
```

```python
from contextlib import ExitStack

import concourse.bass as bass
from concourse import mybir


P = 128
E = 106250
N = 6250
F = 128
HEADS = 4
HID = F // HEADS
EB = 512
CT = EB // P
NB = -(-E // EB)
NB += -NB % CT
EP = NB * EB
T = EP // P
TC = -(-T // P)
TL = T - (TC - 1) * P
NG = -(-N // EB)
NT = NG * CT
NP = NT * P
SLOTS = 4
STRETCH = 8
assert NB % (2 * STRETCH) == 0 and STRETCH * CT * 4 == P
BIG = 3.0e38
FAR = 1.0e6
LN_EPS = 1e-5

ALU = mybir.AluOpType
ACT = mybir.ActivationFunctionType
F32 = mybir.dt.float32
BF16 = mybir.dt.bfloat16
I32 = mybir.dt.int32


def steps(eng, n, unroll, *pieces):
    last = max(lag for lag, _ in pieces)
    head = -(-(last + unroll) // unroll) * unroll
    main = max(head, n - n % unroll)

    def alone(i):
        for lag, f in pieces:
            if 0 <= i - lag < n:
                f((i - lag) // unroll, (i - lag) % unroll)

    for i in range(min(head, n + last)):
        alone(i)
    if main > head:
        with eng.Fori(head // unroll, main // unroll) as r:
            for u in range(unroll):
                for lag, f in pieces:
                    d = u - lag
                    f(r + d // unroll if d // unroll else r, d % unroll)
    for i in range(main, n + last):
        alone(i)


def gnn_program(nc, a, out):
    ctx = ExitStack()

    def sb(name, shape, dt=F32):
        return ctx.enter_context(nc.sbuf_tensor(name, shape, dt))

    def ps(name):
        return ctx.enter_context(nc.psum_tensor(name, [P, EB], F32))

    def sem(name):
        return ctx.enter_context(nc.semaphore(name))

    def dram(name, shape, dt=F32):
        return nc.dram_tensor(name, shape, dt, kind="Internal").ap()

    with ctx:
        meta_d = dram("edge_meta", [4, EP], BF16)
        weight_d = dram("edge_weight_padded", [1, EP])
        dst_d = dram("dst_rows", [T, P])
        last_dst_d = dram("tile_last_dst", [1, T])
        start_d = dram("row_start", [1, NP + P])
        first_d = dram("receiver_rows", [EP, F])
        recv_d = dram("receiver_table", [NP, F])
        send_d = dram("sender_table", [NP, F])
        factor_d = dram("factor_table", [NP, F])
        att_d = dram("attention_table", [NP, F + HEADS])
        scan_d = dram("scan_rows", [EP, F])
        att_scan_d = dram("attention_scan_rows", [EP, F + HEADS])

        ident = sb("ident", [P, P])
        x_nm = sb("x_nm", [P, NT, F])
        xT = sb("xT", [P, NP])
        src_cols = sb("src_cols", [P, T], I32)
        rank_cols = sb("rank_cols", [P, T])
        first_dst = sb("first_dst", [P, TC], I32)
        start_i = sb("start_i", [P, NT], I32)
        end_i = sb("end_i", [P, NT], I32)
        mask = sb("mask", [P, NT])
        inv_deg = sb("inv_deg", [P, NT])
        eps = sb("eps", [P, 1])

        w1 = sb("w1", [P, 2, F]); w1w = sb("w1w", [1, F]); b1 = sb("b1", [P, 1])
        w2 = sb("w2", [P, F]); b2 = sb("b2", [P, F])
        u1 = sb("u1", [P, 2, F]); c1 = sb("c1", [P, 1]); u2 = sb("u2", [P, F]); c2 = sb("c2", [P, F])
        wm = sb("wm", [P, 2, F]); bm = sb("bm", [P, 1]); wc = sb("wc", [P, 2, F]); bc = sb("bc", [P, 1])
        wh = sb("wh", [P, HEADS, HID]); al = sb("al", [P, F]); ar = sb("ar", [P, F])
        w_score = sb("w_score", [P, 2, HEADS])
        w_in = sb("w_in", [P, 2, F]); w_out = sb("w_out", [P, 2, F])

        idx = [sb(f"idx{s}", [P, CT], I32) for s in range(2 * STRETCH)]
        scatter_idx = [sb(f"scatter_idx{s}", [P, CT], I32) for s in range(2)]
        gath_all = sb("gath", [P, 2 * STRETCH, CT, F + HEADS])
        gath = [gath_all[:, s, :, :] for s in range(2 * STRETCH)]
        recv = [sb(f"recv{s}", [P, CT, F]) for s in range(SLOTS)]
        meta = [sb(f"meta{s}", [P, 3, EB], BF16) for s in range(SLOTS)]
        rows = [sb(f"rows{s}", [P, CT, F + HEADS]) for s in range(SLOTS)]
        same = [sb(f"same{s}", [P, CT, P]) for s in range(2)]
        hid = [sb(f"hid{s}", [P, EB]) for s in range(2)]
        scan = [sb(f"scan{s}", [P, EB]) for s in range(2)]
        den = [sb(f"den{s}", [P, EB]) for s in range(2)]
        RT = STRETCH * CT
        NS = NB // STRETCH
        over_head = sb("over_head", [P, RT * P])
        tile_of = sb("tile_of", [P, RT]); head_of = sb("head_of", [P, HEADS]); head_ofT = sb("head_ofT", [HEADS, P])
        bar_c = sb("bar_c", [P, NS, P], BF16); first_c = sb("first_c", [P, NS, P], BF16); last_bar = sb("last_bar", [HEADS, T], BF16)
        small = sb("small", [P, 16, P])
        em, weight_em, sum_em, factor_c = ([small[:, 4 * b + i, :] for b in range(2)] for i in range(4))
        max_in, below_c, drop_c, weight_c, sum_in, left_c, sum_c = (small[:, 8 + i, :] for i in range(7))
        wrow = [small[0:1, 4 * s:4 * s + 4, :].rearrange("p a b -> p (a b)") for s in range(SLOTS)]
        max_c = sb("max_c", [P, P + 1])
        zero_c = sb("zero_c", [P, P]); spread = sb("spread", [P, 2 * RT]); carried = sb("carried", [P, 1])
        max_carry = sb("max_carry", [HEADS, RT + 1]); sum_carry = sb("sum_carry", [HEADS, RT + 1]); last_c = sb("last_c", [HEADS, 2 * RT])
        x_new = [sb(f"x_new{s}", [P, CT, F]) for s in range(2)]
        stats = sb("stats", [P, CT, 6]); mv = [sb(f"mv{s}", [P, CT, 2]) for s in range(2)]; std = [sb(f"std{s}", [P, CT]) for s in range(2)]; rstd = sb("rstd", [P, CT])
        head_sum = sb("head_sum", [P, CT * HEADS])
        bank = [ps(f"bank{k}") for k in range(8)]
        agg, aggT, y_nm, prod = recv[0:2], scan, recv[2:4], [sb(f"prod{s}", [P, EB]) for s in range(2)]
        xT_new, recv_o = den, same
        firsts = x_new

        v_done = sem("v_done")
        a_done = sem("a_done")
        node_got = [sem(f"node_got{s}") for s in range(2)]
        scattered = [sem(f"scattered{s}") for s in range(2)]
        firsts_got = sem("firsts_got")
        n_idx = sem("n_idx")
        n_gath_free = sem("n_gath_free")
        n_agg = sem("n_agg")
        n_agg_free = sem("n_agg_free")
        n_agg_turned = sem("n_agg_turned")
        n_aggT = sem("n_aggT")
        n_hid_ps = sem("n_hid_ps")
        n_hid = sem("n_hid")
        n_rows_ps = sem("n_rows_ps")
        n_rows_free = sem("n_rows_free")
        n_var = sem("n_var")
        n_std = sem("n_std")
        n_x = sem("n_x")
        n_x_turned_a = sem("n_x_turned_a")
        n_x_turned_v = sem("n_x_turned_v")
        n_x_bank_free = sem("n_x_bank_free")
        n_xT_new = sem("n_xT_new")
        n_tab_ps = sem("n_tab_ps")
        n_recv_ps = sem("n_recv_ps")
        n_bank_free = {b: sem(f"n_bank{b}_free") for b in (3, 5, 7)}
        n_heads = sem("n_heads")
        n_tab = sem("n_tab")
        n_recv = sem("n_recv")
        n_recv_sc = sem("n_recv_sc")
        n_stored = [sem(f"n_stored{s}") for s in range(2)]
        n_recv_stored = [sem(f"n_recv_stored{s}") for s in range(2)]
        n_scat_all = sem("n_scat_all")
        n_first_out = sem("n_first_out")
        n_load = sem("n_load"); n_load_ready = sem("n_load_ready")
        out_done = sem("out_done")

        gathered = [sem(f"gathered{s}") for s in range(SLOTS)]
        e_idx = sem("e_idx")
        e_gath_free = sem("e_gath_free")
        recv_in = [sem(f"recv_in{s}") for s in range(SLOTS)]
        meta_in = [sem(f"meta_in{s}") for s in range(SLOTS)]
        e_recv_free = sem("e_recv_free")
        e_meta_free = sem("e_meta_free")
        e_same = sem("e_same"); e_same_free = sem("e_same_free")
        e_pre = sem("e_pre"); e_pre_free = sem("e_pre_free")
        e_hid = sem("e_hid"); e_hid_free = sem("e_hid_free")
        e_msg = sem("e_msg"); e_msg_free = sem("e_msg_free")
        e_scan = sem("e_scan"); e_scan_free = sem("e_scan_free")
        e_back = sem("e_back"); e_back_free = sem("e_back_free")
        e_rows = sem("e_rows")
        stored = [sem(f"stored{s}") for s in range(SLOTS)]
        t_gathered = [sem(f"t_gathered{s}") for s in range(2 * STRETCH)]
        t_idx = sem("t_idx"); t_gath_free = sem("t_gath_free")
        t_marks = sem("t_marks")
        t_er = sem("t_er"); t_er_free = sem("t_er_free")
        t_cb_free = sem("t_cb_free")
        t_em = sem("t_em"); t_last = sem("t_last"); t_carry = sem("t_carry"); t_dlast = sem("t_dlast"); t_dcarry = sem("t_dcarry")
        t_sum = sem("t_sum"); t_weighted = sem("t_weighted")
        t_scoreT = sem("t_scoreT"); t_lastT = sem("t_lastT"); t_carryT = sem("t_carryT"); t_dlastT = sem("t_dlastT")
        t_dcarryT = sem("t_dcarryT")
        t_sumT = sem("t_sumT")
        t_below = sem("t_below"); t_exp_v = sem("t_exp_v")
        t_exp_p = sem("t_exp_p")
        e_idx_free = sem("e_idx_free")

        def part(q, s, unroll, n):
            lo = q * (unroll * n) + s * n
            return slice(lo, lo + n) if isinstance(q, int) else bass.ds(lo, n)

        with ExitStack() as pctx:
            def psb(name, shape, dt=F32):
                return pctx.enter_context(nc.sbuf_tensor(name, shape, dt))

            used = {"gath": 0, "x": 0}

            def carve(where, shape, dt=F32):
                n = shape[0] * (shape[1] if len(shape) > 1 else 1)
                words = n if dt != BF16 else n // 2
                flat = gath_all[:, :, :, :].rearrange("p s c f -> p (s c f)") if where == "gath" else x_nm[:, :, :].rearrange("p t f -> p (t f)")
                t = flat[:, used[where]:used[where] + words]
                used[where] += words
                t = t if dt == F32 else t.bitcast(dt)
                return t.rearrange("p (a b) -> p a b", b=shape[1]) if len(shape) > 1 else t

            dst_r, src_r = carve("x", [TC, P], I32), carve("x", [TC, P], I32)
            prev_r = psb("prev_r", [P, TC], I32)
            prev_f = psb("prev_f", [P, TC])
            goes, bar, rank_b, first_b = (carve("x", [TC, P], BF16) for _ in range(4))
            begins = carve("x", [TC, P])
            dst_f, src_f, rank_f = carve("gath", [TC, P]), carve("gath", [TC, P]), carve("gath", [TC, P])
            zeros = carve("gath", [EP * F // P // (2 * NG)])
            lasts, junk = carve("gath", [T]), (carve("gath", [T]), small[:, :, :].rearrange("p a b -> p (a b)")[:, 0:T])
            node_i = psb("node_i", [P, NT], I32)
            node_f = psb("node_f", [P, NT])
            tail = psb("tail", [1, P])
            tiles = psb("tiles", [P, NT])
            tiles_i = psb("tiles_i", [P, NT], I32)
            inside = psb("inside", [P, NT])
            start_f = psb("start_f", [P, NT])
            end_f = psb("end_f", [P, NT])
            lone = psb("lone", [P, NT])
            start_t = psb("start_t", [NT, P])
            end_t = psb("end_t", [NT, P])
            found = xT[:, :].rearrange("p (t k) -> p t k", k=P)

            filled = sem("prep_filled"); zeroed = sem("prep_zeroed"); zero_ready = sem("prep_zero_ready")
            loaded = sem("prep_loaded"); ident_done = sem("ident_done")
            marked = sem("prep_marked"); written = sem("prep_written"); turned = sem("prep_turned")
            rows_f_ready = sem("prep_rows_f_ready"); p_done = sem("p_done"); turn_free = sem("prep_turn_free")
            dst_written = sem("prep_dst_written"); lasts_in = sem("prep_lasts_in"); tiles_ready = sem("prep_tiles_ready")
            found_in = sem("prep_found_in"); start_ready = sem("prep_start_ready"); start_out = sem("prep_start_out")
            start_written = sem("prep_start_written"); end_in = sem("prep_end_in"); back_ready = sem("prep_back_ready")
            weights_in = sem("weights_in"); heads_ready = sem("prep_heads_ready"); dst_ready = sem("prep_dst_ready"); scores_ready = sem("prep_scores_ready")
            wm_in = sem("wm_in"); fac_in = [sem(f"fac_in{s}") for s in range(SLOTS)]
            fac_last = same[0]; fac_last_ready = sem("fac_last_ready")
            fac_turned = sem("fac_turned"); fac_tab = sem("fac_tab")
            facT = sem("facT"); fac_bank_free = sem("fac_bank_free")
            fac_stored = [sem(f"fac_stored{s}") for s in range(2)]

            full = (TC - 1) * P
            rest = E // P - full
            left = E % P
            with nc.Block() as block:
                @block.sync
                def _(sp):
                    sp.wait_ge(filled, 3)
                    sp.sem_inc(filled, -3)
                    for r, t in ((dst_r, a["dst"]), (src_r, a["src"])):
                        sp.dma_start(r[:, 0:TC - 1, :], t[0:full * P].rearrange("(c p k) -> p c k", p=P, k=P)).then_inc(loaded, 16)
                        sp.dma_start(r[0:rest, TC - 1, :], t[full * P:(full + rest) * P].rearrange("(p k) -> p k", k=P)).then_inc(loaded, 16)
                        sp.dma_start(r[rest:rest + 1, TC - 1, 0:left], t[E - left:E].rearrange("(p k) -> p k", p=1)).then_inc(loaded, 16)
                    with nc.allow_non_contiguous_dma("one word of each tile"):
                        for c in range(TC):
                            lo, n = (1, P - 1) if c == 0 else (0, P if c < TC - 1 else rest + 1)
                            first = (c * P + lo - 1) * P
                            sp.dma_start(prev_r[lo:lo + n, c:c + 1],
                                         a["dst"][first:first + n * P].rearrange("(p k) -> p k", k=P)[:, P - 1:P]).then_inc(loaded, 16)
                    sp.dma_start(wm[:, :, :], a["L1_gnn_Wm"].rearrange("(t p) n -> p t n", p=P)).then_inc(wm_in, 16)
                    for t, src in ((w1[:, 0, :], a["L0_gnn_W1"][0:F, :]), (w1[:, 1, :], a["L0_gnn_W1"][F:2 * F, :]),
                                   (w1w[:, :], a["L0_gnn_W1"][2 * F:2 * F + 1, :]),
                                   (b1[:, :], a["L0_gnn_b1"].rearrange("(p o) -> p o", o=1)),
                                   (w2[:, :], a["L0_gnn_W2"]), (b2[:, :], a["L0_gnn_b2"].partition_broadcast(P)),
                                   (u1[:, :, :], a["L0_gnn_U1"].rearrange("(t p) n -> p t n", p=P)),
                                   (c1[:, :], a["L0_gnn_c1"].rearrange("(p o) -> p o", o=1)),
                                   (u2[:, :], a["L0_gnn_U2"]), (c2[:, :], a["L0_gnn_c2"].partition_broadcast(P)),
                                   (bm[:, :], a["L1_gnn_bm"].rearrange("(p o) -> p o", o=1)),
                                   (wc[:, :, :], a["L1_gnn_Wc"].rearrange("(t p) n -> p t n", p=P)),
                                   (bc[:, :], a["L1_gnn_bc"].rearrange("(p o) -> p o", o=1)),
                                   (wh[:, :, :], a["L2_gnn_W"].rearrange("k f h -> f k h")),
                                   (al[:, :], a["L2_gnn_a_l"].rearrange("k h -> (k h)").partition_broadcast(P)),
                                   (ar[:, :], a["L2_gnn_a_r"].rearrange("k h -> (k h)").partition_broadcast(P)),
                                   (w_in[:, :, :], a["L3_gnn_W_in"].rearrange("t p n -> p t n")),
                                   (w_out[:, :, :], a["L3_gnn_W_out"].rearrange("t p n -> p t n"))):
                        sp.dma_start(t, src).then_inc(weights_in, 16)
                    sp.wait_ge(dst_ready, 1)
                    sp.sem_inc(dst_ready, -1)
                    for c in range(TC):
                        n = P if c < TC - 1 else TL
                        sp.dma_start(dst_d[c * P:c * P + n, :], dst_f[0:n, c, :]).then_inc(dst_written, 16)
                        with nc.allow_non_contiguous_dma("one word of each tile"):
                            sp.dma_start(last_dst_d[0, c * P:c * P + n].rearrange("(p o) -> p o", o=1),
                                         dst_f[0:n, c, P - 1:P]).then_inc(dst_written, 16)
                    sp.wait_ge(dst_written, 32 * TC)
                    sp.sem_inc(dst_written, -32 * TC)
                    sp.dma_start(lasts[:, :], last_dst_d[0, :].partition_broadcast(P)).then_inc(lasts_in, 16)
                    sp.wait_ge(marked, 1)
                    sp.sem_inc(marked, -1)
                    for c in range(TC):
                        n = P if c < TC - 1 else TL
                        at = slice(c * P * P, (c * P + n) * P)
                        for m, r in enumerate((goes, rank_b, bar, first_b)):
                            sp.dma_start(meta_d[m, at].rearrange("(p k) -> p k", k=P), r[0:n, c, :]).then_inc(written, 16)
                    sp.dma_start(weight_d[0:1, E:EP], zeros[0:1, 0:EP - E]).then_inc(written, 16)
                    sp.dma_start(weight_d[0, 0:E].rearrange("(p k) -> p k", k=1250), a["edge_weight"].rearrange("(p k) -> p k", k=1250)).then_inc(written, 16)
                    sp.wait_ge(start_out, 1)
                    sp.sem_inc(start_out, -1)
                    sp.dma_start(start_d[0, 0:NP].rearrange("(t p) -> t p", p=P), start_t[:, :]).then_inc(start_written, 16)
                    sp.dma_start(start_d[0:1, NP:NP + P], tail[:, :]).then_inc(start_written, 16)
                    sp.wait_ge(start_written, 32)
                    sp.sem_inc(start_written, -32)
                    sp.dma_start(end_t[:, :], start_d[0, 1:NP + 1].rearrange("(t p) -> t p", p=P)).then_inc(end_in, 16)
                    sp.wait_ge(written, 16 * (4 * TC + 2))
                    sp.sem_inc(written, -(16 * (4 * TC + 2)))
                    sp.wait_ge(scores_ready, 1)
                    sp.sem_inc(scores_ready, -1)
                    sp.wait_ge(weights_in, 16 * 18)
                    sp.sem_inc(weights_in, -16 * 18)
                    sp.wait_ge(n_load_ready, 1)
                    sp.sem_inc(n_load_ready, -1)
                    whole = N // P
                    sp.dma_start(x_nm[:, 0:whole, :], a["x"][0:whole * P, :].rearrange("(t p) f -> p t f", p=P)).then_inc(n_load, 16)
                    sp.dma_start(x_nm[0:N - whole * P, whole, :], a["x"][whole * P:N, :]).then_inc(n_load, 16)
                    sp.wait_ge(n_load, 32)
                    sp.sem_inc(n_load, -32)
                    for free, n in ((n_gath_free, 2), (n_agg_free, 2), (n_rows_free, 2), (n_x_bank_free, 1), (n_bank_free[7], 1), (n_bank_free[5], 1), (n_bank_free[3], 1),
                                    (e_gath_free, SLOTS), (e_recv_free, SLOTS), (e_meta_free, SLOTS), (e_same_free, 2),
                                    (e_pre_free, 2), (e_hid_free, 2), (e_msg_free, 2), (e_scan_free, 2), (e_back_free, 2),
                                    (t_er_free, 1), (t_cb_free, 1), (t_gath_free, 2 * STRETCH)):
                        sp.sem_inc(free, n)

                @block.scalar
                def _(act):
                    act.wait_ge(zero_ready, 1)
                    act.sem_inc(zero_ready, -1)
                    act.sem_inc(fac_bank_free, 1)
                    fac = a["L1_gnn_factors"]
                    z = first_d.rearrange("(p k r) f -> p k (r f)", p=P, k=2 * NG)

                    def fill(q, s):
                        if not (isinstance(q, int) and q == 0 and s == 0):
                            act.wait_ge(zeroed, 32)
                            act.sem_inc(zeroed, -32)
                        for j in range(2):
                            lo = q * (2 * SLOTS) + (2 * s + j)
                            z_at = z[:, lo:lo + 1, :] if isinstance(q, int) else z[:, bass.ds(lo, 1), :]
                            act.dma_start(z_at, zeros.unsqueeze(1)).then_inc(zeroed, 16)

                    def load(q, s):
                        if isinstance(q, int) and q * SLOTS + s == NG - 1:
                            act.wait_ge(fac_last_ready, 1)
                            act.sem_inc(fac_last_ready, -1)
                            act.dma_start(fac_last[0:N % EB, 0, :], fac[N - N % EB:N, :]).then_inc(fac_in[s], 16)
                        else:
                            act.dma_start(recv[s][:, :, :], fac[part(q, s, SLOTS, EB), :].rearrange("(t p) f -> p t f", p=P)).then_inc(fac_in[s], 16)

                    def keep_turned(q, s):
                        act.wait_ge(fac_turned, 1)
                        act.sem_inc(fac_turned, -1)
                        act.activation(hid[s % 2][:, :], bank[5 + s % 2][:, :], ACT.Copy).then_inc(facT, 1)

                    def store(q, s):
                        if not (isinstance(q, int) and q == 0 and s < 2):
                            act.wait_ge(fac_stored[s % 2], 16)
                            act.sem_inc(fac_stored[s % 2], -16)
                        act.wait_ge(fac_tab, 1)
                        act.sem_inc(fac_tab, -1)
                        act.activation(rows[s % 2][:, :, 0:F], bank[7][:, :].rearrange("p (t f) -> p t f", f=F), ACT.Copy).then_inc(a_done, 1)
                        act.wait_ge(a_done, 1)
                        act.sem_inc(a_done, -1)
                        act.sem_inc(fac_bank_free, 1)
                        act.dma_start(factor_d[part(q, s, SLOTS, EB), :].rearrange("(t p) f -> p t f", p=P), rows[s % 2][:, :, 0:F]).then_inc(fac_stored[s % 2], 16)

                    steps(act, NG, SLOTS, (0, load), (0, fill), (3, keep_turned), (4, store))
                    act.wait_ge(zeroed, 32)
                    act.sem_inc(zeroed, -32)
                    for s in range(2):
                        act.wait_ge(fac_stored[s], 16)
                        act.sem_inc(fac_stored[s], -16)
                    act.wait_ge(fac_bank_free, 1)
                    act.sem_inc(fac_bank_free, -1)

                @block.gpsimd
                def _(pool):
                    pool.memset(dst_r[:, TC - 1, :], N).then_inc(filled, 1)
                    pool.memset(src_r[:, TC - 1, :], 0).then_inc(filled, 1)
                    pool.memset(prev_r[:, 1:TC], N).then_inc(p_done, 1)
                    pool.memset(prev_r[:, 0:1], -1).then_inc(p_done, 1)
                    pool.memset(ident[:, :], 0.0).then_inc(p_done, 1)
                    pool.memset(eps[:, :], LN_EPS).then_inc(p_done, 1)
                    pool.memset(over_head[:, :], 0.0).then_inc(p_done, 1)
                    pool.memset(tail[:, :], float(EP)).then_inc(p_done, 1)
                    pool.iota(node_i[:, :], pattern=[[P, NT]], base=0, channel_multiplier=1).then_inc(p_done, 1)
                    pool.wait_ge(p_done, 7)
                    pool.sem_inc(p_done, -7)
                    pool.sem_inc(filled, 1)
                    pool.affine_select(out=ident[:, :], in_=ident[:, :], compare_op=ALU.not_equal, fill=1.0, base=0,
                                       pattern=[[-1, P]], channel_multiplier=1).then_inc(ident_done, 1)
                    pool.affine_select(out=over_head[:, :], in_=over_head[:, :], compare_op=ALU.not_equal, fill=1.0, base=0,
                                       pattern=[[-1, RT * HEADS], [0, HID]], channel_multiplier=1).then_inc(ident_done, 1)
                    pool.wait_ge(tiles_ready, 1)
                    pool.sem_inc(tiles_ready, -1)
                    for t in range(NT):
                        pool.indirect_dma_start(out=found[:, t, :], out_offset=None, in_=dst_d[:, :],
                                                in_offset=bass.IndirectOffsetOnAxis(ap=tiles_i[:, t:t + 1], axis=0),
                                                bounds_check=T - 1, oob_is_err=False).then_inc(found_in, 16)

                @block.vector
                def _(v):
                    def chain(ins):
                        ins.then_inc(v_done, 1)
                        v.wait_ge(v_done, 1)
                        v.sem_inc(v_done, -1)

                    chain(v.memset(zeros[:, :], 0.0))
                    v.sem_inc(zero_ready, 1)
                    chain(v.memset(fac_last[:, :, :], 0.0))
                    v.sem_inc(fac_last_ready, 1)
                    chain(v.memset(x_nm[:, N // P:NT, :], 0.0))
                    v.sem_inc(n_load_ready, 1)
                    for s in range(2):
                        chain(v.memset(scan[s][:, :], 0.0))
                    chain(v.memset(zero_c[:, :], 0.0))
                    chain(v.memset(max_carry[:, :], 0.0))
                    chain(v.memset(sum_carry[:, :], 0.0))
                    v.wait_ge(loaded, 16 * (6 + TC))
                    v.tensor_copy(dst_f[:, :, :], dst_r[:, :, :]).then_inc(v_done, 1)
                    v.tensor_copy(prev_f[:, :], prev_r[:, :]).then_inc(v_done, 1)
                    v.tensor_copy(first_dst[:, :], dst_r[:, :, 0]).then_inc(v_done, 1)
                    v.tensor_copy(node_f[:, :], node_i[:, :]).then_inc(v_done, 1)
                    v.wait_ge(v_done, 4)
                    v.sem_inc(v_done, -4)
                    v.sem_inc(dst_ready, 1)
                    v.tensor_tensor(goes[:, :, 1:P], dst_f[:, :, 1:P], dst_f[:, :, 0:P - 1], ALU.is_equal).then_inc(v_done, 1)
                    v.tensor_tensor(goes[:, :, 0], dst_f[:, :, 0], prev_f[:, :], ALU.is_equal).then_inc(v_done, 1)
                    v.wait_ge(v_done, 2)
                    v.sem_inc(v_done, -2)
                    chain(v.tensor_scalar(bar[:, :, :], goes[:, :, :], -1.0, BIG, ALU.add, ALU.mult))
                    chain(v.tensor_scalar(begins[:, :, :], goes[:, :, :], -1.0, 1.0, ALU.mult, ALU.add))
                    chain(v.memset(begins[:, :, 0:1], 0.0))
                    for c in range(TC):
                        v.tensor_tensor_scan(rank_f[:, c, :], begins[:, c, :], begins[:, c, :], 0.0, ALU.add, ALU.max).then_inc(v_done, 1)
                    v.wait_ge(v_done, TC)
                    v.sem_inc(v_done, -TC)
                    chain(v.tensor_copy(rank_b[:, :, :], rank_f[:, :, :]))
                    chain(v.tensor_scalar(begins[:, :, :], rank_f[:, :, :], 0.0, None, ALU.is_equal))
                    chain(v.tensor_tensor(begins[:, :, :], begins[:, :, :], goes[:, :, 0:1].to_broadcast([P, TC, P]), ALU.mult))
                    chain(v.tensor_scalar(first_b[:, :, :], begins[:, :, :], -1.0, BIG, ALU.add, ALU.mult))
                    v.sem_inc(marked, 1)
                    chain(v.tensor_copy(src_f[:, :, :], src_r[:, :, :]))
                    v.sem_inc(rows_f_ready, 1)
                    for c in range(TC):
                        n = P if c < TC - 1 else TL
                        v.wait_ge(turned, 1)
                        v.sem_inc(turned, -1)
                        v.tensor_copy(src_cols[:, c * P:c * P + n], bank[c % 2][:, 0:n])
                        v.tensor_copy(rank_cols[:, c * P:c * P + n], bank[c % 2][:, P:P + n]).then_inc(turn_free, 1)
                    v.wait_ge(ident_done, 2)
                    ones_at = over_head[:, :].rearrange("p (t h d) -> p t h d", h=HEADS, d=HID)[:, :, :, 0]
                    chain(v.reduce_sum(tile_of[:, :], ones_at, mybir.AxisListType.X))
                    chain(v.reduce_sum(head_of[:, :], ones_at.rearrange("p t h -> p h t"), mybir.AxisListType.X))
                    v.sem_inc(heads_ready, 1)
                    v.wait_ge(turned, 1)
                    v.sem_inc(turned, -1)
                    chain(v.tensor_copy(head_ofT[:, :], bank[4][0:HEADS, 0:P]))
                    v.wait_ge(weights_in, 16 * 18)
                    for m, w in enumerate((al, ar)):
                        by_head = w[:, :].rearrange("p (h d) -> p h d", h=HEADS)
                        chain(v.tensor_tensor(by_head, by_head, wh[:, :, :], ALU.mult))
                        chain(v.reduce_sum(w_score[:, m, :], by_head, mybir.AxisListType.X))
                    v.sem_inc(scores_ready, 1)
                    v.wait_ge(lasts_in, 16)
                    v.sem_inc(v_done, 1)
                    with v.Fori(0, NT // 2) as q:
                        for u in range(2):
                            v.wait_ge(v_done, 1)
                            v.sem_inc(v_done, -1)
                            v.tensor_scalar(junk[u][:, :], lasts[:, :], node_f[:, bass.ds(q * 2 + u, 1)], None, ALU.is_lt, ALU.add,
                                            accum_out=tiles[:, bass.ds(q * 2 + u, 1)]).then_inc(v_done, 1)
                    v.wait_ge(v_done, 1)
                    v.sem_inc(v_done, -1)
                    chain(v.tensor_scalar(tiles[:, :], tiles[:, :], float(T - 1), None, ALU.min))
                    chain(v.tensor_copy(tiles_i[:, :], tiles[:, :]))
                    v.sem_inc(tiles_ready, 1)
                    v.wait_ge(found_in, 16 * NT)
                    v.sem_inc(v_done, 1)
                    with v.Fori(0, NT // 2) as q:
                        for u in range(2):
                            v.wait_ge(v_done, 1)
                            v.sem_inc(v_done, -1)
                            v.tensor_scalar(junk[u][:, 0:P], found[:, bass.ds(q * 2 + u, 1), :], node_f[:, bass.ds(q * 2 + u, 1)], None, ALU.is_lt, ALU.add,
                                            accum_out=inside[:, bass.ds(q * 2 + u, 1)]).then_inc(v_done, 1)
                    v.wait_ge(v_done, 1)
                    v.sem_inc(v_done, -1)
                    chain(v.scalar_tensor_tensor(start_f[:, :], tiles[:, :], float(P), inside[:, :], ALU.mult, ALU.add))
                    v.sem_inc(start_ready, 1)
                    v.wait_ge(turned, 1)
                    v.sem_inc(turned, -1)
                    chain(v.tensor_copy(start_t[:, :], bank[2][0:NT, 0:P]))
                    v.sem_inc(start_out, 1)
                    v.wait_ge(turned, 1)
                    v.sem_inc(turned, -1)
                    chain(v.tensor_copy(end_f[:, :], bank[3][:, 0:NT]))
                    chain(v.tensor_tensor(lone[:, :], end_f[:, :], start_f[:, :], ALU.subtract))
                    chain(v.tensor_scalar(mask[:, :], lone[:, :], 1.0, None, ALU.min))
                    chain(v.tensor_scalar(inv_deg[:, :], lone[:, :], 1.0, None, ALU.max))
                    chain(v.reciprocal(inv_deg[:, :], inv_deg[:, :]))
                    chain(v.tensor_tensor(inv_deg[:, :], inv_deg[:, :], mask[:, :], ALU.mult))
                    chain(v.tensor_scalar(end_f[:, :], end_f[:, :], -1.0, 0.0, ALU.add, ALU.max))
                    chain(v.tensor_copy(end_i[:, :], end_f[:, :]))
                    chain(v.tensor_scalar(lone[:, :], mask[:, :], -FAR, FAR, ALU.mult, ALU.add))
                    chain(v.tensor_tensor(lone[:, :], lone[:, :], start_f[:, :], ALU.add))
                    chain(v.tensor_copy(start_i[:, :], lone[:, :]))

                @block.tensor
                def _(pe):
                    pe.wait_ge(ident_done, 2)
                    pe.wait_ge(rows_f_ready, 1)
                    pe.sem_inc(rows_f_ready, -1)
                    for c in range(TC):
                        if c >= 2:
                            pe.wait_ge(turn_free, 1)
                            pe.sem_inc(turn_free, -1)
                        pe.transpose(bank[c % 2][:, 0:P], src_f[:, c, :], ident[:, :])
                        pe.transpose(bank[c % 2][:, P:2 * P], rank_f[:, c, :], ident[:, :]).then_inc(turned, 1)
                    pe.wait_ge(heads_ready, 1)
                    pe.sem_inc(heads_ready, -1)
                    pe.transpose(bank[4][0:HEADS, 0:P], head_of[:, :], ident[:, :]).then_inc(turned, 1)
                    pe.wait_ge(wm_in, 16)
                    pe.sem_inc(wm_in, -16)

                    def turn(q, s):
                        pe.wait_ge(fac_in[s], 16)
                        pe.sem_inc(fac_in[s], -16)
                        t = fac_last if isinstance(q, int) and q * SLOTS + s == NG - 1 else recv[s]
                        for c in range(CT):
                            ins = pe.transpose(bank[5 + s % 2][:, c * P:(c + 1) * P], t[:, c, :], ident[:, :])
                        ins.then_inc(fac_turned, 1)

                    def product(q, s):
                        pe.wait_ge(facT, 1)
                        pe.sem_inc(facT, -1)
                        pe.wait_ge(fac_bank_free, 1)
                        pe.sem_inc(fac_bank_free, -1)
                        for c in range(CT):
                            ins = pe.matmul(bank[7][:, c * P:(c + 1) * P], hid[s % 2][:, c * P:(c + 1) * P], wm[:, 1, :], start=True, stop=True)
                        ins.then_inc(fac_tab, 1)

                    steps(pe, NG, SLOTS, (0, turn), (1, product))
                    pe.wait_ge(start_ready, 1)
                    pe.sem_inc(start_ready, -1)
                    pe.transpose(bank[2][0:NT, 0:P], start_f[:, :], ident[:, :]).then_inc(turned, 1)
                    pe.wait_ge(end_in, 16)
                    pe.sem_inc(end_in, -16)
                    pe.transpose(bank[3][:, 0:NT], end_t[:, :], ident[0:NT, 0:NT]).then_inc(turned, 1)
                    pe.wait_ge(turn_free, 2)
                    pe.sem_inc(turn_free, -2)

        started = {"node": 0, "scatter": 0, "firsts": 0, "edge": 0}

        def node_phase(k):
            gathers = 1 <= k <= 5
            dense = k in (1, 2, 4, 5)
            norm = k in (1, 2, 3, 5)
            turn = k in (0, 1, 2, 3)
            makes_recv = k in (0, 1, 2)
            by_matmul = k in (0, 1, 2)
            wx, wa = {1: (u1[:, 0, :], u1[:, 1, :]), 2: (wc[:, 0, :], wc[:, 1, :]), 4: (w_in[:, 0, :], w_in[:, 1, :]),
                      5: (w_out[:, 0, :], w_out[:, 1, :])}.get(k, (None, None))
            back = u2 if k == 1 else ident
            w_tab = {0: w1[:, 0, :], 2: wh[:, :, :].rearrange("p k h -> p (k h)")}.get(k)
            w_recv = {0: w1[:, 1, :], 1: wm[:, 0, :], 2: w_score[:, :, :].rearrange("p m h -> p (m h)")}.get(k)
            width = F + HEADS if k == 3 else F
            from_d = att_scan_d if k == 3 else scan_d
            to_d = {0: send_d, 2: att_d, 3: send_d, 4: send_d}.get(k)
            to_w = F + HEADS if k == 2 else F
            agg_ps, hid_ps, rows_ps, x_ps, tab_ps = bank[0:2], (bank[2], bank[2]), bank[4:6], bank[6], bank[7]
            recv_bank = {0: 5, 2: 3}.get(k, 7)
            late = 3 if dense else 1
            new = late + norm
            got_before, scattered_before = started["node"], started["scatter"]
            groups = [(NG + 1 - s) // 2 for s in range(2)]

            with nc.Block() as block:
                @block.gpsimd
                def _(pool):
                    def gather(q, s):
                        pool.wait_ge(n_gath_free, 1)
                        pool.sem_inc(n_gath_free, -1)
                        pool.tensor_copy(idx[s][:, :], end_i[:, part(q, s, 2, CT)]).then_inc(n_idx, 1)
                        pool.wait_ge(n_idx, 1)
                        pool.sem_inc(n_idx, -1)
                        for c in range(CT):
                            pool.indirect_dma_start(out=gath[s][:, c, 0:width], out_offset=None, in_=from_d[:, :],
                                                    in_offset=bass.IndirectOffsetOnAxis(ap=idx[s][:, c:c + 1], axis=0),
                                                    bounds_check=EP - 1, oob_is_err=False).then_inc(node_got[s], 16)

                    def scatter(q, s):
                        pool.wait_ge(n_recv_sc, 1)
                        pool.sem_inc(n_recv_sc, -1)
                        pool.tensor_copy(scatter_idx[s][:, :], start_i[:, part(q, s, 2, CT)]).then_inc(n_idx, 1)
                        pool.wait_ge(n_idx, 1)
                        pool.sem_inc(n_idx, -1)
                        for c in range(CT):
                            pool.indirect_dma_start(out=first_d[:, :],
                                                    out_offset=bass.IndirectOffsetOnAxis(ap=scatter_idx[s][:, c:c + 1], axis=0),
                                                    in_=recv_o[s][:, c, :], in_offset=None,
                                                    bounds_check=EP - 1, oob_is_err=False).then_inc(scattered[s], 16)

                    work = [(8 if gathers else 0, scatter)] * makes_recv + [(0, gather)] * gathers
                    if work:
                        steps(pool, NG, 2, *work)

                @block.sync
                def _(sp):
                    def store_table(q, s):
                        sp.wait_ge(n_tab, 1)
                        sp.sem_inc(n_tab, -1)
                        rows_d = to_d[part(q, s, 2, EB), :].rearrange("(t p) f -> p t f", p=P)
                        rows_s = {3: x_new, 4: y_nm}.get(k, rows)[s][:, :, 0:to_w]
                        sp.dma_start(rows_d, rows_s).then_inc(n_stored[s], 16)

                    def store_receivers(q, s):
                        sp.wait_ge(n_recv, 1)
                        sp.sem_inc(n_recv, -1)
                        sp.dma_start(recv_d[part(q, s, 2, EB), :].rearrange("(t p) f -> p t f", p=P), recv_o[s][:, :, :]).then_inc(n_recv_stored[s], 16)

                    work = [(0, store_table)] * (to_d is not None) + [(0, store_receivers)] * makes_recv
                    if work:
                        steps(sp, NG, 2, *work)
                    if k == 5:
                        sp.wait_ge(n_tab, NG)
                        sp.sem_inc(n_tab, -NG)
                        whole = N // P
                        sp.dma_start(out[0:whole * P, :].rearrange("(t p) f -> p t f", p=P), x_nm[:, 0:whole, :]).then_inc(out_done, 16)
                        sp.dma_start(out[whole * P:N, :], x_nm[0:N - whole * P, whole, :]).then_inc(out_done, 16)
                        sp.wait_ge(out_done, 32)

                @block.vector
                def _(v):
                    def chain(ins, n=1):
                        ins.then_inc(v_done, 1)
                        v.wait_ge(v_done, n)
                        v.sem_inc(v_done, -n)

                    def tiled(t):
                        return t[:, :].rearrange("p (t f) -> p t f", f=F)

                    def aggregate(q, s):
                        if dense:
                            v.wait_ge(n_agg_free, 1)
                            v.sem_inc(n_agg_free, -1)
                        v.wait_ge(node_got[s], (q + 1) * (16 * CT) + 16 * CT * got_before * groups[s])
                        tile_mask = mask[:, part(q, s, 2, CT)].unsqueeze(2)
                        g, o = gath[s][:, :, 0:F], agg[s][:, :, :]
                        if k == 1:
                            chain(v.tensor_tensor(o, g, b2[:, :].unsqueeze(1).to_broadcast([P, CT, F]), ALU.add))
                            chain(v.tensor_tensor(o, o, tile_mask.to_broadcast([P, CT, F]), ALU.mult))
                        elif k == 3:
                            h = head_sum[:, :].rearrange("p (t h) -> p t h", h=HEADS)
                            chain(v.tensor_scalar(h, gath[s][:, :, F:F + HEADS], 1e-16, None, ALU.add))
                            chain(v.reciprocal(h, h))
                            chain(v.tensor_tensor(h, h, tile_mask.to_broadcast([P, CT, HEADS]), ALU.mult))
                            for c in range(CT):
                                ins = v.tensor_tensor(o[:, c, :].rearrange("p (h d) -> p h d", h=HEADS), g[:, c, :].rearrange("p (h d) -> p h d", h=HEADS),
                                                      h[:, c, :].unsqueeze(2).to_broadcast([P, HEADS, HID]), ALU.mult)
                                ins.then_inc(v_done, 1)
                            v.wait_ge(v_done, CT)
                            v.sem_inc(v_done, -CT)
                        else:
                            if k in (4, 5):
                                tile_mask = inv_deg[:, part(q, s, 2, CT)].unsqueeze(2)
                            chain(v.tensor_tensor(o, g, tile_mask.to_broadcast([P, CT, F]), ALU.mult))
                        v.sem_inc(n_gath_free, 1)
                        if dense:
                            v.sem_inc(n_agg, 1)

                    def update(q, s):
                        x, y, new = x_nm[:, part(q, s, 2, CT), :], y_nm[s][:, :, :], x_new[s][:, :, :]
                        if not gathers:
                            chain(v.tensor_copy(new, x))
                            v.sem_inc(n_x, 1)
                            return
                        if k == 4 and not (isinstance(q, int) and q == 0):
                            v.wait_ge(n_stored[s], 16)
                            v.sem_inc(n_stored[s], -16)
                        if dense:
                            v.wait_ge(n_rows_ps, 1)
                            v.sem_inc(n_rows_ps, -1)
                        r = tiled(rows_ps[s])
                        if k == 1:
                            chain(v.tensor_tensor(y, r, c2[:, :].unsqueeze(1).to_broadcast([P, CT, F]), ALU.add))
                            chain(v.tensor_tensor(y, x, y, ALU.add))
                        elif k == 2:
                            chain(v.tensor_tensor(y, x, r, ALU.add))
                            chain(v.tensor_tensor(y, x, y, ALU.add))
                        elif k == 3:
                            chain(v.tensor_tensor(y, x, agg[s][:, :, :], ALU.add))
                        elif k == 4:
                            chain(v.tensor_copy(y, r))
                            v.sem_inc(n_tab, 1)
                        else:
                            chain(v.tensor_tensor(y, x, r, ALU.add))
                        if dense:
                            v.sem_inc(n_rows_free, 1)
                        if not norm:
                            return
                        for c in range(CT):
                            v.bn_stats(stats[:, c, :], y[:, c, :]).then_inc(v_done, 1)
                        v.wait_ge(v_done, CT)
                        v.sem_inc(v_done, -CT)
                        for c in range(CT):
                            v.bn_aggr(mv[s][:, c, :], stats[:, c, :]).then_inc(n_var, 1)

                    def normalize(q, s):
                        x, y, new = x_nm[:, part(q, s, 2, CT), :], y_nm[s][:, :, :], x_new[s][:, :, :]
                        v.wait_ge(n_std, 1)
                        v.sem_inc(n_std, -1)
                        chain(v.reciprocal(rstd[:, :], std[s][:, :]))
                        if k == 3 and not (isinstance(q, int) and q == 0):
                            v.wait_ge(n_stored[s], 16)
                            v.sem_inc(n_stored[s], -16)
                        for c in range(CT):
                            v.tensor_scalar(new[:, c, :], y[:, c, :], mv[s][:, c, 0:1], rstd[:, c:c + 1], ALU.subtract, ALU.mult).then_inc(v_done, 1)
                        v.wait_ge(v_done, CT)
                        v.sem_inc(v_done, -CT)
                        if turn:
                            v.sem_inc(n_x, 1)
                        chain(v.tensor_copy(x, new))
                        if k in (3, 5):
                            v.sem_inc(n_tab, 1)

                    def keep_xT(q, s):
                        v.wait_ge(n_x_turned_v, 1)
                        v.sem_inc(n_x_turned_v, -1)
                        chain(v.tensor_copy(xT[:, part(q, s, 2, EB)], xT_new[s][:, :]))

                    def receivers(q, s):
                        if not (isinstance(q, int) and q == 0):
                            v.wait_ge(n_recv_stored[s], 16)
                            v.sem_inc(n_recv_stored[s], -16)
                            v.wait_ge(scattered[s], q * (16 * CT) + 16 * CT * scattered_before * groups[s])
                        if k != 2:
                            v.wait_ge(n_recv_ps, 1)
                            v.sem_inc(n_recv_ps, -1)
                            chain(v.tensor_copy(recv_o[s][:, :, :], tiled(bank[recv_bank])))
                            v.sem_inc(n_bank_free[recv_bank], 1)
                        else:
                            v.wait_ge(n_heads, 1)
                            v.sem_inc(n_heads, -1)
                            v.wait_ge(n_recv_ps, 1)
                            v.sem_inc(n_recv_ps, -1)
                            e = bank[recv_bank][:, 0:2 * CT * HEADS].rearrange("p (t m h) -> p m t h", t=CT, m=2)
                            v.tensor_copy(rows[s][:, :, F:F + HEADS], e[:, 0, :, :]).then_inc(v_done, 1)
                            for c in range(CT):
                                v.tensor_copy(recv_o[s][:, c, :].rearrange("p (h d) -> p h d", d=HID),
                                              e[:, 1, c, :].unsqueeze(2).to_broadcast([P, HEADS, HID])).then_inc(v_done, 1)
                            v.wait_ge(v_done, 1 + CT)
                            v.sem_inc(v_done, -(1 + CT))
                            v.sem_inc(n_bank_free[recv_bank], 1)
                            v.sem_inc(n_tab, 1)
                        v.sem_inc(n_recv, 1)
                        v.sem_inc(n_recv_sc, 1)

                    work = [(new + 3, receivers)] * makes_recv + [(new + 2, keep_xT)] * turn + [(late + 1, normalize)] * norm + [(late, update)] + [(0, aggregate)] * gathers
                    steps(v, NG, 2, *work)
                    if k in (3, 4):
                        for s in range(2):
                            v.wait_ge(n_stored[s], 16)
                            v.sem_inc(n_stored[s], -16)
                    if makes_recv:
                        for s in range(2):
                            v.wait_ge(n_recv_stored[s], 16)
                            v.sem_inc(n_recv_stored[s], -16)

                @block.scalar
                def _(act):
                    def chain(ins):
                        ins.then_inc(a_done, 1)
                        act.wait_ge(a_done, 1)
                        act.sem_inc(a_done, -1)

                    def keep_aggT(q, s):
                        act.wait_ge(n_agg_turned, 1)
                        act.sem_inc(n_agg_turned, -1)
                        act.sem_inc(n_agg_free, 1)
                        act.activation(aggT[s][:, :], agg_ps[s][:, :], ACT.Copy).then_inc(n_aggT, 1)

                    def hidden(q, s):
                        act.wait_ge(n_hid_ps, 1)
                        act.sem_inc(n_hid_ps, -1)
                        if k == 5:
                            chain(act.activation(hid[s][:, :], hid_ps[s][:, :], ACT.Copy))
                        elif k == 4:
                            chain(act.activation(hid[s][:, :], hid_ps[s][:, :], ACT.Relu))
                            chain(act.activation(xT[:, part(q, s, 2, EB)], hid_ps[s][:, :], ACT.Relu))
                        else:
                            chain(act.activation(hid[s][:, :], hid_ps[s][:, :], ACT.Relu, bias=(c1 if k == 1 else bc)[:, 0:1]))
                        act.sem_inc(n_hid, 1)

                    def deviation(q, s):
                        act.wait_ge(n_var, CT)
                        act.sem_inc(n_var, -CT)
                        act.activation(std[s][:, :], mv[s][:, :, 1], ACT.Sqrt, bias=eps[:, 0:1]).then_inc(n_std, 1)

                    def turned_x(q, s):
                        act.wait_ge(n_x_turned_a, 1)
                        act.sem_inc(n_x_turned_a, -1)
                        chain(act.activation(xT_new[s][:, :], x_ps[:, :], ACT.Copy))
                        act.sem_inc(n_x_bank_free, 1)
                        act.sem_inc(n_x_turned_v, 1)
                        if by_matmul:
                            act.sem_inc(n_xT_new, 1)

                    def table(q, s):
                        if not (isinstance(q, int) and q == 0):
                            act.wait_ge(n_stored[s], 16)
                            act.sem_inc(n_stored[s], -16)
                        act.wait_ge(n_tab_ps, 1)
                        act.sem_inc(n_tab_ps, -1)
                        chain(act.activation(rows[s][:, :, 0:F], tab_ps[:, :].rearrange("p (t f) -> p t f", f=F), ACT.Copy))
                        act.sem_inc(n_bank_free[7], 1)
                        act.sem_inc(n_heads if k == 2 else n_tab, 1)

                    work = ([(new + 2, table)] * (w_tab is not None) + [(new + 1, turned_x)] * turn + [(late, deviation)] * norm
                            + [(1, hidden), (0, keep_aggT)] * dense)
                    steps(act, NG, 2, *work)
                    if w_tab is not None:
                        for s in range(2):
                            act.wait_ge(n_stored[s], 16)
                            act.sem_inc(n_stored[s], -16)

                @block.tensor
                def _(pe):
                    def turn_agg(q, s):
                        pe.wait_ge(n_agg, 1)
                        pe.sem_inc(n_agg, -1)
                        for c in range(CT):
                            ins = pe.transpose(agg_ps[s][:, c * P:(c + 1) * P], agg[s][:, c, :], ident[:, :])
                        ins.then_inc(n_agg_turned, 1)

                    def product(q, s):
                        pe.wait_ge(n_aggT, 1)
                        pe.sem_inc(n_aggT, -1)
                        pe.matmul(hid_ps[s][:, :], wa, aggT[s][:, :], start=True, stop=False)
                        pe.matmul(hid_ps[s][:, :], wx, xT[:, part(q, s, 2, EB)], start=False, stop=True).then_inc(n_hid_ps, 1)

                    def product_rows(q, s):
                        pe.wait_ge(n_hid, 1)
                        pe.sem_inc(n_hid, -1)
                        pe.wait_ge(n_rows_free, 1)
                        pe.sem_inc(n_rows_free, -1)
                        for c in range(CT):
                            ins = pe.matmul(rows_ps[s][:, c * P:(c + 1) * P], hid[s][:, c * P:(c + 1) * P], back[:, :], start=True, stop=True)
                        ins.then_inc(n_rows_ps, 1)

                    def turn_x(q, s):
                        pe.wait_ge(n_x, 1)
                        pe.sem_inc(n_x, -1)
                        pe.wait_ge(n_x_bank_free, 1)
                        pe.sem_inc(n_x_bank_free, -1)
                        for c in range(CT):
                            ins = pe.transpose(x_ps[:, c * P:(c + 1) * P], x_new[s][:, c, :], ident[:, :])
                        ins.then_inc(n_x_turned_a, 1)

                    def tables(q, s):
                        pe.wait_ge(n_xT_new, 1)
                        pe.sem_inc(n_xT_new, -1)
                        for w, b, ready in ((w_tab, 7, n_tab_ps), (w_recv, recv_bank, n_recv_ps)):
                            if w is None:
                                continue
                            pe.wait_ge(n_bank_free[b], 1)
                            pe.sem_inc(n_bank_free[b], -1)
                            n = 2 * HEADS if b == 3 else F
                            for c in range(CT):
                                ins = pe.matmul(bank[b][:, c * n:(c + 1) * n], xT_new[s][:, c * P:(c + 1) * P], w, start=True, stop=True)
                            ins.then_inc(ready, 1)

                    work = ([(new + 2, tables)] * by_matmul + [(new + 1, turn_x)] * turn
                            + [(2, product_rows), (1, product), (0, turn_agg)] * dense)
                    steps(pe, NG, 2, *work)
            if gathers:
                started["node"] += 1
            if makes_recv:
                started["scatter"] += 1

        def edge_phase(k):
            expands = k <= 2
            table = factor_d if k == 2 else send_d
            marks = {1: (1, 3), 2: (0, 2)}.get(k, (0, 1))
            pre_ps, msg_ps, back_ps = bank[0:2], bank[2:4], bank[4:6]
            before = started["edge"]
            firsts_before, scatters = started["firsts"], started["scatter"]

            rounds = NB // SLOTS

            with nc.Block() as block:
                @block.gpsimd
                def _(pool):
                    if expands:
                        for c in range(TC):
                            pool.indirect_dma_start(out=firsts[c // CT][:, c % CT, :], out_offset=None, in_=recv_d[:, :],
                                                    in_offset=bass.IndirectOffsetOnAxis(ap=first_dst[:, c:c + 1], axis=0),
                                                    bounds_check=NP - 1, oob_is_err=False).then_inc(firsts_got, 16)

                    def gather(q, s):
                        pool.wait_ge(e_idx, 1)
                        pool.sem_inc(e_idx, -1)
                        pool.wait_ge(e_gath_free, 1)
                        pool.sem_inc(e_gath_free, -1)
                        for c in range(CT):
                            pool.indirect_dma_start(out=gath[s][:, c, 0:F], out_offset=None, in_=table[:, :],
                                                    in_offset=bass.IndirectOffsetOnAxis(ap=idx[s][:, c:c + 1], axis=0),
                                                    bounds_check=NP - 1, oob_is_err=False).then_inc(gathered[s], 16)

                    steps(pool, NB, SLOTS, (0, gather))

                @block.sync
                def _(sp):
                    if expands:
                        sp.wait_ge(n_scat_all, 1)
                        sp.sem_inc(n_scat_all, -1)
                        sp.wait_ge(firsts_got, 16 * (firsts_before + TC))
                        by_tile = first_d.rearrange("(t e) f -> t e f", e=P)
                        for c in range(TC):
                            n = P if c < TC - 1 else TL
                            sp.dma_start(by_tile[c * P:c * P + n, 0, :], firsts[c // CT][0:n, c % CT, :]).then_inc(n_first_out, 16)
                        sp.wait_ge(n_first_out, 16 * TC)
                        sp.sem_inc(n_first_out, -16 * TC)

                    def load(q, s):
                        sp.wait_ge(e_meta_free, 1)
                        sp.sem_inc(e_meta_free, -1)
                        lo, hi = marks
                        sp.dma_start(meta[s][:, lo:hi, :], meta_d[lo:hi, part(q, s, SLOTS, EB)].partition_broadcast(P)).then_inc(meta_in[s], 16)
                        if expands:
                            sp.wait_ge(e_recv_free, 1)
                            sp.sem_inc(e_recv_free, -1)
                            sp.dma_start(recv[s][:, :, :], first_d[part(q, s, SLOTS, EB), :].rearrange("(c p) f -> p c f", p=P)).then_inc(recv_in[s], 16)
                            if k == 1:
                                sp.dma_start(wrow[s][:, :], weight_d[:, part(q, s, SLOTS, EB)]).then_inc(recv_in[s], 16)

                    def store(q, s):
                        sp.wait_ge(e_rows, 1)
                        sp.sem_inc(e_rows, -1)
                        sp.dma_start(scan_d[part(q, s, SLOTS, EB), :].rearrange("(c p) f -> p c f", p=P), rows[s][:, :, 0:F]).then_inc(stored[s], 16)

                    steps(sp, NB, SLOTS, (0, load), (5, store))

                @block.tensor
                def _(pe):
                    def senders(q, s):
                        if expands:
                            pe.wait_ge(recv_in[s], 32 if k == 1 else 16)
                            pe.sem_inc(recv_in[s], -(32 if k == 1 else 16))
                            pe.wait_ge(e_same, 1)
                            pe.sem_inc(e_same, -1)
                        pe.wait_ge(e_pre_free, 1)
                        pe.sem_inc(e_pre_free, -1)
                        pe.wait_ge(gathered[s], (q + 1) * (16 * CT) + 16 * CT * rounds * before)
                        b, g = pre_ps[s % 2], gath[s]
                        if k >= 4:
                            for c in range(CT):
                                ins = pe.transpose(b[:, c * P:(c + 1) * P], g[:, c, 0:F], ident[:, :])
                            ins.then_inc(e_pre, 1)
                            return
                        if k == 1:
                            pe.matmul(b[:, :], w1w[:, :], wrow[s][:, :], start=True, stop=False)
                        for c in range(CT):
                            o = b[:, c * P:(c + 1) * P]
                            pe.matmul(o, g[:, c, 0:F], ident[:, :], start=k != 1, stop=False)
                            ins = pe.matmul(o, recv[s][:, c, :], same[s % 2][:, c, :], start=False, stop=k != 1 or c == CT - 1)
                        ins.then_inc(e_pre, 1)

                    def message(q, s):
                        pe.wait_ge(e_hid, 1)
                        pe.sem_inc(e_hid, -1)
                        pe.wait_ge(e_msg_free, 1)
                        pe.sem_inc(e_msg_free, -1)
                        pe.matmul(msg_ps[s % 2][:, :], w2[:, :], hid[s % 2][:, :], start=True, stop=True).then_inc(e_msg, 1)

                    def turn_back(q, s):
                        pe.wait_ge(e_scan, 1)
                        pe.sem_inc(e_scan, -1)
                        pe.wait_ge(e_back_free, 1)
                        pe.sem_inc(e_back_free, -1)
                        for c in range(CT):
                            ins = pe.transpose(back_ps[s % 2][:, c * P:(c + 1) * P], scan[s % 2][:, c * P:(c + 1) * P], ident[:, :])
                        ins.then_inc(e_back, 1)

                    steps(pe, NB, SLOTS, (0, senders), *[(1, message)] * (k == 1), (3 if expands else 2, turn_back))

                @block.scalar
                def _(act):
                    def chain(ins):
                        ins.then_inc(a_done, 1)
                        act.wait_ge(a_done, 1)
                        act.sem_inc(a_done, -1)

                    def indices(q, s):
                        act.activation(idx[s][:, :], src_cols[:, part(q, s, SLOTS, CT)], ACT.Copy).then_inc(e_idx, 1)

                    def hidden(q, s):
                        act.wait_ge(e_pre, 1)
                        act.sem_inc(e_pre, -1)
                        act.sem_inc(e_gath_free, 1)
                        act.sem_inc(e_recv_free, 1)
                        act.sem_inc(e_same_free, 1)
                        act.wait_ge(e_hid_free, 1)
                        act.sem_inc(e_hid_free, -1)
                        chain(act.activation(hid[s % 2][:, :], pre_ps[s % 2][:, :], ACT.Relu, bias=(b1 if k == 1 else bm)[:, 0:1]))
                        act.sem_inc(e_pre_free, 1)
                        act.sem_inc(e_hid, 1)

                    def keep_rows(q, s):
                        act.wait_ge(e_back, 1)
                        act.sem_inc(e_back, -1)
                        act.sem_inc(e_scan_free, 1)
                        if not (isinstance(q, int) and q == 0):
                            act.wait_ge(stored[s], 16)
                            act.sem_inc(stored[s], -16)
                        ins = act.activation(rows[s][:, :, 0:F], back_ps[s % 2][:, :].rearrange("p (c f) -> p c f", f=F), ACT.Copy)
                        chain(ins)
                        act.sem_inc(e_back_free, 1)
                        act.sem_inc(e_rows, 1)

                    def read(q, s):
                        act.wait_ge(e_idx_free, 1)
                        act.sem_inc(e_idx_free, -1)

                    first = hidden if expands else read
                    steps(act, NB, SLOTS, (4, first), (0, indices), (7 if expands else 5, keep_rows))
                    for s in range(SLOTS):
                        act.wait_ge(stored[s], 16)
                        act.sem_inc(stored[s], -16)

                @block.vector
                def _(v):
                    if expands:
                        for s in range(2):
                            v.wait_ge(scattered[s], 16 * CT * scatters * ((NG + 1 - s) // 2))
                        v.sem_inc(n_scat_all, 1)

                    def chain(ins):
                        ins.then_inc(v_done, 1)
                        v.wait_ge(v_done, 1)
                        v.sem_inc(v_done, -1)

                    def same_receiver(q, s):
                        v.wait_ge(meta_in[s], 16)
                        v.sem_inc(meta_in[s], -16)
                        v.wait_ge(e_same_free, 1)
                        v.sem_inc(e_same_free, -1)
                        v.tensor_tensor(same[s % 2][:, :, :], meta[s][:, 1, :].rearrange("p (c e) -> p c e", e=P),
                                        rank_cols[:, part(q, s, SLOTS, CT)].unsqueeze(2).to_broadcast([P, CT, P]), ALU.is_equal).then_inc(e_same, 1)

                    def reduce(q, s):
                        if k >= 4:
                            v.wait_ge(meta_in[s], 16)
                            v.sem_inc(meta_in[s], -16)
                        v.wait_ge({1: e_msg, 2: e_hid}.get(k, e_pre), 1)
                        v.sem_inc({1: e_msg, 2: e_hid}.get(k, e_pre), -1)
                        if k == 1:
                            v.sem_inc(e_hid_free, 1)
                        if k >= 4:
                            v.sem_inc(e_gath_free, 1)
                            v.sem_inc(e_idx_free, 1)
                        v.wait_ge(e_scan_free, 1)
                        v.sem_inc(e_scan_free, -1)
                        src = {1: msg_ps, 2: hid}.get(k, pre_ps)[s % 2][:, :]
                        go_on = meta[s][:, 2 if k == 1 else 0, :]
                        chain(v.tensor_tensor_scan(scan[s % 2][:, :], go_on, src, scan[1 - s % 2][:, EB - 1:EB],
                                                   ALU.add if k == 1 else ALU.mult, ALU.max if k == 1 else ALU.add))
                        v.sem_inc({1: e_msg_free, 2: e_hid_free}.get(k, e_pre_free), 1)
                        v.sem_inc(e_meta_free, 1)
                        v.sem_inc(e_scan, 1)

                    if expands:
                        steps(v, NB, SLOTS, (0, same_receiver), (2, reduce))
                    else:
                        steps(v, NB, SLOTS, (0, reduce))
            started["edge"] += 1

        def attention_phase():
            U, SB = 2 * STRETCH, STRETCH
            fac_ps, wv_ps, back_ps, er_ps, cb = bank[0:2], bank[2:4], bank[4:6], bank[6], bank[7]
            R = SB * CT

            firsts_before, scatters = started["firsts"], started["scatter"]
            with nc.Block() as block:
                @block.gpsimd
                def _(pool):
                    for c in range(TC):
                        pool.indirect_dma_start(out=firsts[c // CT][:, c % CT, :], out_offset=None, in_=recv_d[:, :],
                                                in_offset=bass.IndirectOffsetOnAxis(ap=first_dst[:, c:c + 1], axis=0),
                                                bounds_check=NP - 1, oob_is_err=False).then_inc(firsts_got, 16)

                    def gather(q, s):
                        pool.wait_ge(t_idx, 1)
                        pool.sem_inc(t_idx, -1)
                        pool.wait_ge(t_gath_free, 1)
                        pool.sem_inc(t_gath_free, -1)
                        for c in range(CT):
                            pool.indirect_dma_start(out=gath[s][:, c, :], out_offset=None, in_=att_d[:, :],
                                                    in_offset=bass.IndirectOffsetOnAxis(ap=idx[s][:, c:c + 1], axis=0),
                                                    bounds_check=NP - 1, oob_is_err=False).then_inc(t_gathered[s], 16)

                    steps(pool, NB, U, (0, gather))

                @block.sync
                def _(sp):
                    sp.wait_ge(n_scat_all, 1)
                    sp.sem_inc(n_scat_all, -1)
                    sp.wait_ge(firsts_got, 16 * (firsts_before + TC))
                    by_tile = first_d.rearrange("(t e) f -> t e f", e=P)
                    for c in range(TC):
                        n = P if c < TC - 1 else TL
                        sp.dma_start(by_tile[c * P:c * P + n, 0, :], firsts[c // CT][0:n, c % CT, :]).then_inc(n_first_out, 16)
                    sp.wait_ge(n_first_out, 16 * TC)
                    sp.sem_inc(n_first_out, -16 * TC)

                    for h in range(HEADS):
                        for t, m in ((bar_c, 2), (first_c, 3)):
                            sp.dma_start(t[h::HEADS, :, :], meta_d[m, :].rearrange("(b t e) -> t b e", t=R, e=P)).then_inc(t_marks, 16)
                    with nc.allow_non_contiguous_dma("one word of each tile"):
                        sp.dma_start(last_bar[:, :], meta_d[3, :].rearrange("(t e) -> t e", e=P)[:, P - 1].partition_broadcast(HEADS)).then_inc(t_marks, 16)

                    def load(q, s):
                        sp.wait_ge(e_meta_free, 1)
                        sp.sem_inc(e_meta_free, -1)
                        sp.dma_start(meta[s % SLOTS][:, 1:2, :], meta_d[1:2, part(q, s, U, EB)].partition_broadcast(P)).then_inc(meta_in[s % SLOTS], 16)
                        sp.wait_ge(e_recv_free, 1)
                        sp.sem_inc(e_recv_free, -1)
                        sp.dma_start(recv[s % SLOTS][:, :, :], first_d[part(q, s, U, EB), :].rearrange("(c p) f -> p c f", p=P)).then_inc(recv_in[s % SLOTS], 16)

                    def store(q, s):
                        sp.wait_ge(e_rows, 1)
                        sp.sem_inc(e_rows, -1)
                        sp.dma_start(att_scan_d[part(q, s, U, EB), :].rearrange("(c p) f -> p c f", p=P), rows[s % SLOTS][:, :, :]).then_inc(stored[s % SLOTS], 16)

                    steps(sp, NB, U, (0, load), (13, store))

                @block.tensor
                def _(pe):
                    def receiver_scores(q, s):
                        pe.wait_ge(recv_in[s % SLOTS], 16)
                        pe.sem_inc(recv_in[s % SLOTS], -16)
                        pe.wait_ge(e_same, 1)
                        pe.sem_inc(e_same, -1)
                        pe.wait_ge(t_er_free, 1)
                        pe.sem_inc(t_er_free, -1)
                        for c in range(CT):
                            ins = pe.matmul(er_ps[:, c * HEADS:(c + 1) * HEADS], same[s % 2][:, c, :], recv[s % SLOTS][:, c, 0:F:HID], start=True, stop=True)
                        ins.then_inc(t_er, 1)

                    def stretch(q, s):
                        if s % SB != SB - 1:
                            return
                        b = s // SB
                        pe.wait_ge(t_em, 1)
                        pe.sem_inc(t_em, -1)
                        pe.wait_ge(t_cb_free, 1)
                        pe.sem_inc(t_cb_free, -1)
                        pe.transpose(cb[:, 0:P], em[b][:, :], ident[:, :]).then_inc(t_scoreT, 1)
                        pe.wait_ge(t_last, 1)
                        pe.sem_inc(t_last, -1)
                        pe.matmul(cb[0:HEADS, P:P + R], head_of[:, :], spread[:, 0:R], start=True, stop=True).then_inc(t_lastT, 1)
                        pe.wait_ge(t_carry, 1)
                        pe.sem_inc(t_carry, -1)
                        pe.matmul(cb[:, 160:160 + R], head_ofT[:, :], max_carry[:, 0:R], start=True, stop=True).then_inc(t_carryT, 1)
                        pe.wait_ge(t_exp_p, 1)
                        pe.sem_inc(t_exp_p, -1)
                        pe.transpose(cb[:, 192:192 + P], weight_c[:, :], ident[:, :])
                        pe.wait_ge(t_dlast, 1)
                        pe.sem_inc(t_dlast, -1)
                        pe.matmul(cb[0:HEADS, 320:320 + 2 * R], head_of[:, :], spread[:, 0:2 * R], start=True, stop=True).then_inc(t_dlastT, 1)
                        pe.wait_ge(t_dcarry, 1)
                        pe.sem_inc(t_dcarry, -1)
                        pe.matmul(cb[:, 384:384 + R], head_ofT[:, :], sum_carry[:, 0:R], start=True, stop=True).then_inc(t_dcarryT, 1)
                        pe.wait_ge(t_sum, 1)
                        pe.sem_inc(t_sum, -1)
                        pe.transpose(cb[:, 0:P], sum_c[:, :], ident[:, :]).then_inc(t_sumT, 1)

                    def turn_weighted(q, s):
                        pe.wait_ge(e_msg_free, 1)
                        pe.sem_inc(e_msg_free, -1)
                        pe.wait_ge(t_weighted, 1)
                        pe.sem_inc(t_weighted, -1)
                        for c in range(CT):
                            ins = pe.transpose(wv_ps[s % 2][:, c * P:(c + 1) * P], gath[s][:, c, 0:F], ident[:, :])
                        ins.then_inc(e_msg, 1)
                        pe.wait_ge(e_pre_free, 1)
                        pe.sem_inc(e_pre_free, -1)
                        for c in range(CT):
                            t = (s % SB) * CT + c
                            ins = pe.matmul(fac_ps[s % 2][:, c * P:(c + 1) * P], over_head[:, t * P:(t + 1) * P], factor_c[s // SB][:, :], start=True, stop=True)
                        ins.then_inc(e_pre, 1)

                    def turn_back(q, s):
                        pe.wait_ge(e_scan, 1)
                        pe.sem_inc(e_scan, -1)
                        pe.wait_ge(e_back_free, 1)
                        pe.sem_inc(e_back_free, -1)
                        for c in range(CT):
                            ins = pe.transpose(back_ps[s % 2][:, c * P:(c + 1) * P], scan[s % 2][:, c * P:(c + 1) * P], ident[:, :])
                        ins.then_inc(e_back, 1)

                    steps(pe, NB, U, (9, turn_weighted), (11, turn_back), (0, receiver_scores), (1, stretch))

                @block.scalar
                def _(act):
                    def chain(ins):
                        ins.then_inc(a_done, 1)
                        act.wait_ge(a_done, 1)
                        act.sem_inc(a_done, -1)

                    def indices(q, s):
                        act.activation(idx[s][:, :], src_cols[:, part(q, s, U, CT)], ACT.Copy).then_inc(t_idx, 1)

                    def stretch(q, s):
                        if s % SB != SB - 1:
                            return
                        b = s // SB
                        act.wait_ge(t_below, 1)
                        act.sem_inc(t_below, -1)
                        act.activation(weight_c[:, :], below_c[:, :], ACT.Exp, scale=-1.0).then_inc(a_done, 1)
                        act.activation(factor_c[b][:, :], drop_c[:, :], ACT.Exp, scale=-1.0).then_inc(a_done, 1)
                        act.wait_ge(a_done, 2)
                        act.sem_inc(a_done, -2)
                        act.sem_inc(t_exp_p, 1)
                        act.sem_inc(t_exp_v, 1)
                        act.wait_ge(t_sumT, 1)
                        act.sem_inc(t_sumT, -1)
                        chain(act.activation(sum_em[b][:, :], cb[:, 0:P], ACT.Copy))
                        act.sem_inc(t_cb_free, 1)

                    def keep_weighted(q, s):
                        act.wait_ge(e_msg, 1)
                        act.sem_inc(e_msg, -1)
                        act.sem_inc(t_gath_free, 1)
                        act.wait_ge(e_hid_free, 1)
                        act.sem_inc(e_hid_free, -1)
                        chain(act.activation(hid[s % 2][:, :], wv_ps[s % 2][:, :], ACT.Copy))
                        act.sem_inc(e_msg_free, 1)
                        act.sem_inc(e_hid, 1)

                    def keep_rows(q, s):
                        act.wait_ge(e_back, 1)
                        act.sem_inc(e_back, -1)
                        act.sem_inc(e_scan_free, 1)
                        if not (isinstance(q, int) and q * U + s < SLOTS):
                            act.wait_ge(stored[s % SLOTS], 16)
                            act.sem_inc(stored[s % SLOTS], -16)
                        act.activation(rows[s % SLOTS][:, :, 0:F], back_ps[s % 2][:, :].rearrange("p (c f) -> p c f", f=F), ACT.Copy).then_inc(a_done, 1)
                        lo = (s % SB) * CT * HEADS
                        act.activation(rows[s % SLOTS][:, :, F:F + HEADS], sum_em[s // SB][:, lo:lo + CT * HEADS].rearrange("p (c h) -> p c h", h=HEADS), ACT.Copy).then_inc(a_done, 1)
                        act.wait_ge(a_done, 2)
                        act.sem_inc(a_done, -2)
                        act.sem_inc(e_back_free, 1)
                        act.sem_inc(e_rows, 1)

                    steps(act, NB, U, (9 + 7, keep_weighted), (11 + 7, keep_rows), (0, indices), (1 + 7, stretch))
                    for s in range(SLOTS):
                        act.wait_ge(stored[s], 16)
                        act.sem_inc(stored[s], -16)

                @block.vector
                def _(v):
                    for s in range(2):
                        v.wait_ge(scattered[s], 16 * CT * scatters * ((NG + 1 - s) // 2))
                    v.sem_inc(n_scat_all, 1)

                    def chain(ins):
                        ins.then_inc(v_done, 1)
                        v.wait_ge(v_done, 1)
                        v.sem_inc(v_done, -1)

                    v.wait_ge(t_marks, 16 * (2 * HEADS + 1))
                    v.sem_inc(t_marks, -(16 * (2 * HEADS + 1)))

                    def same_receiver(q, s):
                        v.wait_ge(meta_in[s % SLOTS], 16)
                        v.sem_inc(meta_in[s % SLOTS], -16)
                        v.wait_ge(e_same_free, 1)
                        v.sem_inc(e_same_free, -1)
                        v.tensor_tensor(same[s % 2][:, :, :], meta[s % SLOTS][:, 1, :].rearrange("p (c e) -> p c e", e=P),
                                        rank_cols[:, part(q, s, U, CT)].unsqueeze(2).to_broadcast([P, CT, P]), ALU.is_equal).then_inc(e_same, 1)

                    def scores(q, s):
                        v.wait_ge(t_er, 1)
                        v.sem_inc(t_er, -1)
                        v.sem_inc(e_recv_free, 1)
                        v.sem_inc(e_same_free, 1)
                        v.sem_inc(e_meta_free, 1)
                        lo = (s % SB) * CT * HEADS
                        v.wait_ge(t_gathered[s], (q + 1) * (16 * CT))
                        chain(v.tensor_tensor(em[s // SB][:, lo:lo + CT * HEADS].rearrange("p (c h) -> p c h", h=HEADS),
                                              gath[s][:, :, F:F + HEADS], er_ps[:, 0:CT * HEADS].rearrange("p (c h) -> p c h", h=HEADS), ALU.add))
                        v.sem_inc(t_er_free, 1)

                    def stretch(q, s):
                        if s % SB != SB - 1:
                            return
                        b = s // SB
                        bar, first = bar_c[:, part(q, b, 2, 1), :].rearrange("p o e -> p (o e)"), first_c[:, part(q, b, 2, 1), :].rearrange("p o e -> p (o e)")
                        chain(v.scalar_tensor_tensor(em[b][:, :], em[b][:, :], 0.2, em[b][:, :], ALU.mult, ALU.max))
                        v.sem_inc(t_em, 1)
                        v.wait_ge(t_scoreT, 1)
                        v.sem_inc(t_scoreT, -1)
                        scoreT = cb[:, 0:P]
                        chain(v.tensor_tensor_scan(max_in[:, :], bar, scoreT, -BIG, ALU.add, ALU.max))
                        chain(v.tensor_scalar(spread[:, 0:R], tile_of[:, :], max_in[:, P - 1:P], None, ALU.mult))
                        v.sem_inc(t_last, 1)
                        v.wait_ge(t_lastT, 1)
                        v.sem_inc(t_lastT, -1)
                        chain(v.tensor_tensor_scan(max_carry[:, 1:R + 1], last_bar[:, part(q, b, 2, R)], cb[0:HEADS, P:P + R], max_carry[:, 0:1], ALU.add, ALU.max))
                        v.sem_inc(t_carry, 1)
                        v.wait_ge(t_carryT, 1)
                        v.sem_inc(t_carryT, -1)
                        chain(v.tensor_tensor(spread[:, 0:R], cb[:, 160:160 + R], tile_of[:, :], ALU.mult))
                        v.reduce_sum(max_c[:, 0:1], spread[:, 0:R], mybir.AxisListType.X).then_inc(v_done, 1)
                        v.tensor_copy(max_carry[:, 0:1], max_carry[:, R:R + 1]).then_inc(v_done, 1)
                        v.wait_ge(v_done, 2)
                        v.sem_inc(v_done, -2)
                        chain(v.scalar_tensor_tensor(max_c[:, 1:P + 1], first, max_c[:, 0:1], max_in[:, :], ALU.add, ALU.max))
                        v.scalar_tensor_tensor(below_c[:, :], max_c[:, 1:P + 1], -1e9, scoreT, ALU.max, ALU.subtract).then_inc(v_done, 1)
                        v.scalar_tensor_tensor(drop_c[:, :], max_c[:, 0:P], -1e9, bar, ALU.max, ALU.add).then_inc(v_done, 1)
                        v.wait_ge(v_done, 2)
                        v.sem_inc(v_done, -2)
                        chain(v.scalar_tensor_tensor(drop_c[:, :], max_c[:, 1:P + 1], -1e9, drop_c[:, :], ALU.max, ALU.subtract))
                        v.sem_inc(t_below, 1)
                        v.wait_ge(t_exp_v, 1)
                        v.sem_inc(t_exp_v, -1)
                        v.tensor_tensor_scan(sum_in[:, :], factor_c[b][:, :], weight_c[:, :], 0.0, ALU.mult, ALU.add).then_inc(v_done, 1)
                        v.tensor_tensor_scan(left_c[:, :], factor_c[b][:, :], zero_c[:, :], 1.0, ALU.mult, ALU.add).then_inc(v_done, 1)
                        v.wait_ge(v_done, 2)
                        v.sem_inc(v_done, -2)
                        v.tensor_scalar(spread[:, 0:R], tile_of[:, :], sum_in[:, P - 1:P], None, ALU.mult).then_inc(v_done, 1)
                        v.tensor_scalar(spread[:, R:2 * R], tile_of[:, :], left_c[:, P - 1:P], None, ALU.mult).then_inc(v_done, 1)
                        v.wait_ge(v_done, 2)
                        v.sem_inc(v_done, -2)
                        v.sem_inc(t_dlast, 1)
                        v.wait_ge(t_dlastT, 1)
                        v.sem_inc(t_dlastT, -1)
                        v.tensor_copy(weight_em[b][:, :], cb[:, 192:192 + P]).then_inc(v_done, 1)
                        v.tensor_copy(last_c[:, :], cb[0:HEADS, 320:320 + 2 * R]).then_inc(v_done, 1)
                        v.wait_ge(v_done, 2)
                        v.sem_inc(v_done, -2)
                        chain(v.tensor_tensor_scan(sum_carry[:, 1:R + 1], last_c[:, R:2 * R], last_c[:, 0:R], sum_carry[:, 0:1], ALU.mult, ALU.add))
                        v.sem_inc(t_dcarry, 1)
                        v.wait_ge(t_dcarryT, 1)
                        v.sem_inc(t_dcarryT, -1)
                        chain(v.tensor_tensor(spread[:, 0:R], cb[:, 384:384 + R], tile_of[:, :], ALU.mult))
                        v.reduce_sum(carried[:, :], spread[:, 0:R], mybir.AxisListType.X).then_inc(v_done, 1)
                        v.tensor_copy(sum_carry[:, 0:1], sum_carry[:, R:R + 1]).then_inc(v_done, 1)
                        v.wait_ge(v_done, 2)
                        v.sem_inc(v_done, -2)
                        chain(v.scalar_tensor_tensor(sum_c[:, :], left_c[:, :], carried[:, 0:1], sum_in[:, :], ALU.mult, ALU.add))
                        v.sem_inc(t_sum, 1)

                    def weigh(q, s):
                        lo = (s % SB) * CT * HEADS
                        w = weight_em[s // SB][:, lo:lo + CT * HEADS].rearrange("p (c h) -> p c h", h=HEADS).unsqueeze(3).to_broadcast([P, CT, HEADS, HID])
                        wh_rows = gath[s][:, :, 0:F].rearrange("p c (h d) -> p c h d", h=HEADS)
                        v.tensor_tensor(wh_rows, wh_rows, w, ALU.mult).then_inc(t_weighted, 1)

                    def add_up(q, s):
                        v.wait_ge(e_pre, 1)
                        v.sem_inc(e_pre, -1)
                        v.wait_ge(e_hid, 1)
                        v.sem_inc(e_hid, -1)
                        v.wait_ge(e_scan_free, 1)
                        v.sem_inc(e_scan_free, -1)
                        chain(v.tensor_tensor_scan(scan[s % 2][:, :], fac_ps[s % 2][:, :], hid[s % 2][:, :], scan[1 - s % 2][:, EB - 1:EB], ALU.mult, ALU.add))
                        v.sem_inc(e_pre_free, 1)
                        v.sem_inc(e_hid_free, 1)
                        v.sem_inc(e_scan, 1)

                    steps(v, NB, U, (9, weigh), (10, add_up), (0, same_receiver), (1, scores), (1, stretch))

        node_phase(0)
        for k in range(1, 6):
            if k == 3:
                attention_phase()
            else:
                edge_phase(k)
            if k <= 3:
                started["firsts"] += TC
            node_phase(k)


_INS = ['x', 'src', 'dst', 'edge_weight', 'L0_gnn_W1', 'L0_gnn_b1', 'L0_gnn_W2', 'L0_gnn_b2', 'L0_gnn_U1', 'L0_gnn_c1',
        'L0_gnn_U2', 'L0_gnn_c2', 'L1_gnn_factors', 'L1_gnn_Wm', 'L1_gnn_bm', 'L1_gnn_Wc', 'L1_gnn_bc', 'L2_gnn_W',
        'L2_gnn_a_l', 'L2_gnn_a_r', 'L3_gnn_W_in', 'L3_gnn_W_out']


def kernel(**inputs):
    import numpy as _np
    import concourse.bacc as _bacc
    from concourse import mybir as _mybir
    from concourse.bass_utils import run_bass_kernel_spmd as _run

    nc = _bacc.Bacc("TRN2", target_bir_lowering=False, num_devices=1)
    arrays, args = {}, {}
    for name in _INS:
        array = _np.ascontiguousarray(inputs[name])
        arrays[f"in_{name}_dram"] = array
        args[name] = nc.dram_tensor(f"in_{name}_dram", array.shape, _mybir.dt.from_np(array.dtype), kind="ExternalInput").ap()
    out = nc.dram_tensor("out_0_dram", (N, F), F32, kind="ExternalOutput").ap()
    gnn_program(nc, args, out)
    r = _run(nc, [arrays], core_ids=[0])
    return r.results[0]["out_0_dram"]
```
